# Optimizing a Trainium2 kernel written in Bass

```python
import numpy as np
import jax
import jax.numpy as jnp

def _softmax(x, axis=-1):
    return jax.nn.softmax(x, axis=axis)

def _gelu(x):
    return jax.nn.gelu(x, approximate=True)

def _silu(x):
    return jax.nn.silu(x)

def _sigmoid(x):
    return jax.nn.sigmoid(x)

def _layernorm(x, axis=-1, eps=1e-05):
    m = jnp.mean(x, axis=axis, keepdims=True)
    v = jnp.var(x, axis=axis, keepdims=True)
    return (x - m) / jnp.sqrt(v + eps)

def _scatter_add(tgt, idx, src, axis=0):
    return tgt.at[idx].add(src)

def _segment_sum(src, seg, n):
    return jax.ops.segment_sum(src, seg, n)
kernel_name = 'mk_decoder_postln_d2_seqx_r4_c6a919'

def setup_inputs(seed: int=0):
    np.random.seed(seed)
    _w = jnp.asarray

    def _rec_inputs():
        import jax
        import jax.numpy as jnp
        _rk = jax.random.key(seed)
        x = -0.0003929 + 0.9999 * jax.random.normal(jax.random.fold_in(_rk, 1), (32, 100, 256), jnp.float32)
        _lenS = 100 - jax.random.randint(jax.random.fold_in(_rk, 7), (32,), 0, max(1, 100 // 4) + 1, jnp.int32)
        _lenS2 = 361 - jax.random.randint(jax.random.fold_in(_rk, 8), (32,), 0, max(1, 361 // 4) + 1, jnp.int32)
        _ctx_1024P = jax.random.normal(jax.random.fold_in(_rk, 11), (32, 16, 256), jnp.float32)
        _ctx_1024c = jax.random.dirichlet(jax.random.fold_in(_rk, 511), 0.3 * jnp.ones((16,), jnp.float32), (32, 361))
        _ctx_1024t = jnp.einsum('bsk,bkd->bsd', _ctx_1024c, _ctx_1024P)
        _ctx_1024t = _ctx_1024t * jax.lax.rsqrt(jnp.mean(jnp.square(_ctx_1024t)) + 1e-12) * 0.953939
        ctx_1024 = 2.81802e-05 + 1.00001 * (_ctx_1024t + 0.3 * jax.random.normal(jax.random.fold_in(_rk, 611), (32, 361, 256), jnp.float32))
        _validS = jnp.arange(100)[None, :] < _lenS[:, None]
        _validS2 = jnp.arange(361)[None, :] < _lenS2[:, None]
        _causal = jnp.tril(jnp.ones((100, 100), dtype=bool))
        mask_BxSxS2_ff1 = jnp.where(jnp.ones((32, 100, 361), dtype=bool), 1.0, 0.0).astype(jnp.float32)
        mask_BxS2_ff1 = jnp.where(jnp.ones((32, 361), dtype=bool), 1.0, 0.0).astype(jnp.float32)
        return (x, ctx_1024, mask_BxSxS2_ff1, mask_BxS2_ff1)
    x, ctx_1024, mask_BxSxS2_ff1, mask_BxS2_ff1 = _rec_inputs()

    def _L0_attn_setup():
        import jax, jax.numpy as jnp
        import numpy as np
        B, N, C = (8, 1024, 256)
        key = jax.random.key(seed)
        k1, k2, k3 = jax.random.split(key, 3)
        x = jax.random.normal(k1, (B, N, C), dtype=jnp.float32)
        w_qkv = jax.random.normal(k2, (3 * C, C), dtype=jnp.float32) * C ** (-0.5)
        w_conv1 = jax.random.normal(k3, (C,), dtype=jnp.float32) * C ** (-0.5)
        return {'x': x, 'w_qkv': w_qkv, 'w_conv1': w_conv1}
    _L0_attn_all = _L0_attn_setup()
    _L0_attn_in = {k: v for k, v in _L0_attn_all.items() if k in ('w_qkv', 'w_conv1')}
    del _L0_attn_all

    def _L0_xattn_setup():
        import jax, jax.numpy as jnp
        import numpy as np
        key = jax.random.key(seed)
        ks = jax.random.split(key, 5)
        B, S, D = (8, 512, 256)
        return {'query': jax.random.normal(ks[0], (B, S, D), dtype=jnp.float32), 'key': jax.random.normal(ks[1], (B, S, D), dtype=jnp.float32), 'value': jax.random.normal(ks[2], (B, S, D), dtype=jnp.float32), 'cell_mask': jnp.ones((B, S, S), dtype=jnp.float32), 'seq_mask': jnp.ones((B, S), dtype=jnp.float32), 'W_k': jax.random.normal(ks[3], (D, D), dtype=jnp.float32) * (1.0 / np.sqrt(D)), 'b_k': jnp.zeros((D,), dtype=jnp.float32), 'W_o': jax.random.normal(ks[4], (D, D), dtype=jnp.float32) * (1.0 / np.sqrt(D)), 'b_o': jnp.zeros((D,), dtype=jnp.float32)}
    _L0_xattn_all = _L0_xattn_setup()
    _L0_xattn_in = {k: v for k, v in _L0_xattn_all.items() if k in ('W_k', 'b_k', 'W_o', 'b_o')}
    del _L0_xattn_all

    def _L0_ffn_setup():
        import jax, jax.numpy as jnp
        import numpy as np
        CAPACITY_FACTOR = 0.5
        NUM_HEADS = 16
        key = jax.random.key(seed)
        ks = jax.random.split(key, 6)
        B, N, D = (4, 1024, 256)
        s = 1.0 / np.sqrt(D)
        return {'token_inputs': jax.random.normal(ks[0], (B, N, D), jnp.float32), 'Wg': jax.random.normal(ks[1], (D, 1), jnp.float32) * s, 'Wq': jax.random.normal(ks[2], (D, D), jnp.float32) * s, 'Wk': jax.random.normal(ks[3], (D, D), jnp.float32) * s, 'Wv': jax.random.normal(ks[4], (D, D), jnp.float32) * s, 'Wo': jax.random.normal(ks[5], (D, D), jnp.float32) * s}
    _L0_ffn_all = _L0_ffn_setup()
    _L0_ffn_in = {k: v for k, v in _L0_ffn_all.items() if k in ('Wg', 'Wq', 'Wk', 'Wv', 'Wo')}
    del _L0_ffn_all

    def _L1_attn_setup():
        import jax, jax.numpy as jnp
        import numpy as np
        EMBED_DIM = 256
        NUM_HEADS = 16
        HEAD_DIM = EMBED_DIM // NUM_HEADS
        WINDOW_SIZE = 32
        HALF_BAND = 2 * WINDOW_SIZE
        BAND = 2 * HALF_BAND + 1
        key = jax.random.key(seed)
        ks = jax.random.split(key, 9)
        B, T, E = (1, 256, EMBED_DIM)
        scale = 0.02
        return {'hidden_states': jax.random.normal(ks[0], (B, T, E), jnp.float32), 'Wq': jax.random.normal(ks[1], (E, E), jnp.float32) * scale, 'bq': jax.random.normal(ks[2], (E,), jnp.float32) * scale, 'Wk': jax.random.normal(ks[3], (E, E), jnp.float32) * scale, 'bk': jax.random.normal(ks[4], (E,), jnp.float32) * scale, 'Wv': jax.random.normal(ks[5], (E, E), jnp.float32) * scale, 'bv': jax.random.normal(ks[6], (E,), jnp.float32) * scale, 'Wo': jax.random.normal(ks[7], (E, E), jnp.float32) * scale, 'bo': jax.random.normal(ks[8], (E,), jnp.float32) * scale}
    _L1_attn_all = _L1_attn_setup()
    _L1_attn_in = {k: v for k, v in _L1_attn_all.items() if k in ('Wq', 'bq', 'Wk', 'bk', 'Wv', 'bv', 'Wo', 'bo')}
    del _L1_attn_all

    def _L1_xattn_setup():
        import jax, jax.numpy as jnp
        import numpy as np
        D = 256
        key = jax.random.key(seed)
        ks = jax.random.split(key, 11)
        B, Sq, Skv = (4, 512, 512)
        s = 0.02
        return {'query': jax.random.normal(ks[0], (B, Sq, D), jnp.float32), 'key': jax.random.normal(ks[1], (B, Skv, D), jnp.float32), 'value': jax.random.normal(ks[2], (B, Skv, D), jnp.float32), 'Wq': jax.random.normal(ks[3], (D, D), jnp.float32) * s, 'bq': jnp.zeros((D,), jnp.float32), 'Wk': jax.random.normal(ks[4], (D, D), jnp.float32) * s, 'bk': jnp.zeros((D,), jnp.float32), 'Wv': jax.random.normal(ks[5], (D, D), jnp.float32) * s, 'bv': jnp.zeros((D,), jnp.float32), 'Wo': jax.random.normal(ks[6], (D, D), jnp.float32) * s, 'bo': jnp.zeros((D,), jnp.float32)}
    _L1_xattn_all = _L1_xattn_setup()
    _L1_xattn_in = {k: v for k, v in _L1_xattn_all.items() if k in ('Wq', 'bq', 'Wk', 'bk', 'Wv', 'bv', 'Wo', 'bo')}
    del _L1_xattn_all

    def _L1_ffn_setup():
        import jax, jax.numpy as jnp
        import numpy as np
        EPS_RMS = 1e-06
        EPS_ACT = 1e-05

        def simple_rms_norm(x):
            ms = jnp.mean(jnp.square(x), axis=-1, keepdims=True)
            return x * jax.lax.rsqrt(ms + EPS_RMS)

        def activation_quant(x):
            absmax = jnp.max(jnp.abs(jax.lax.stop_gradient(x)), axis=-1, keepdims=True)
            scale = 127.0 / jnp.clip(absmax, EPS_ACT, None)
            q = jnp.clip(jnp.round(x * scale), -128.0, 127.0) / scale
            return x + jax.lax.stop_gradient(q - x)
        key = jax.random.key(seed)
        k1, k2, k3 = jax.random.split(key, 3)
        B, S, D_IN, D_OUT = (8, 2048, 256, 256)
        x = jax.random.normal(k1, (B, S, D_IN), dtype=jnp.float32)
        w_int8 = jax.random.randint(k2, (D_OUT, D_IN), -128, 128, dtype=jnp.int32)
        weight_scale = jnp.float32(127.0 / 0.06)
        bias = jax.random.normal(k3, (D_OUT,), dtype=jnp.float32) * 0.01
        return {'x': x, 'w_int8': w_int8, 'weight_scale': weight_scale, 'bias': bias}
    _L1_ffn_all = _L1_ffn_setup()
    _L1_ffn_in = {k: v for k, v in _L1_ffn_all.items() if k in ('w_int8', 'weight_scale', 'bias')}
    del _L1_ffn_all
    return {'x': x, 'ctx_1024': ctx_1024, 'mask_BxSxS2_ff1': mask_BxSxS2_ff1, 'mask_BxS2_ff1': mask_BxS2_ff1, 'L0_attn_w_qkv': _L0_attn_in['w_qkv'], 'L0_attn_w_conv1': _L0_attn_in['w_conv1'], 'L0_xattn_W_k': _L0_xattn_in['W_k'], 'L0_xattn_b_k': _L0_xattn_in['b_k'], 'L0_xattn_W_o': _L0_xattn_in['W_o'], 'L0_xattn_b_o': _L0_xattn_in['b_o'], 'L0_ffn_Wg': _L0_ffn_in['Wg'], 'L0_ffn_Wq': _L0_ffn_in['Wq'], 'L0_ffn_Wk': _L0_ffn_in['Wk'], 'L0_ffn_Wv': _L0_ffn_in['Wv'], 'L0_ffn_Wo': _L0_ffn_in['Wo'], 'L1_attn_Wq': _L1_attn_in['Wq'], 'L1_attn_bq': _L1_attn_in['bq'], 'L1_attn_Wk': _L1_attn_in['Wk'], 'L1_attn_bk': _L1_attn_in['bk'], 'L1_attn_Wv': _L1_attn_in['Wv'], 'L1_attn_bv': _L1_attn_in['bv'], 'L1_attn_Wo': _L1_attn_in['Wo'], 'L1_attn_bo': _L1_attn_in['bo'], 'L1_xattn_Wq': _L1_xattn_in['Wq'], 'L1_xattn_bq': _L1_xattn_in['bq'], 'L1_xattn_Wk': _L1_xattn_in['Wk'], 'L1_xattn_bk': _L1_xattn_in['bk'], 'L1_xattn_Wv': _L1_xattn_in['Wv'], 'L1_xattn_bv': _L1_xattn_in['bv'], 'L1_xattn_Wo': _L1_xattn_in['Wo'], 'L1_xattn_bo': _L1_xattn_in['bo'], 'L1_ffn_w_int8': _L1_ffn_in['w_int8'], 'L1_ffn_weight_scale': _L1_ffn_in['weight_scale'], 'L1_ffn_bias': _L1_ffn_in['bias']}

def reference(x, ctx_1024, mask_BxSxS2_ff1, mask_BxS2_ff1, L0_attn_w_qkv, L0_attn_w_conv1, L0_xattn_W_k, L0_xattn_b_k, L0_xattn_W_o, L0_xattn_b_o, L0_ffn_Wg, L0_ffn_Wq, L0_ffn_Wk, L0_ffn_Wv, L0_ffn_Wo, L1_attn_Wq, L1_attn_bq, L1_attn_Wk, L1_attn_bk, L1_attn_Wv, L1_attn_bv, L1_attn_Wo, L1_attn_bo, L1_xattn_Wq, L1_xattn_bq, L1_xattn_Wk, L1_xattn_bk, L1_xattn_Wv, L1_xattn_bv, L1_xattn_Wo, L1_xattn_bo, L1_ffn_w_int8, L1_ffn_weight_scale, L1_ffn_bias):
    import jax
    import jax.numpy as jnp

    def _L0_attn_ref(x, w_qkv, w_conv1):
        import jax, jax.numpy as jnp
        import numpy as np
        B, N, C = (8, 1024, 256)
        b, n, c = x.shape
        scale = c ** (-0.5)
        qkv = jnp.einsum('bnc,dc->bnd', x, w_qkv)
        q = qkv[..., :c]
        k = qkv[..., c:2 * c]
        v = qkv[..., 2 * c:]
        agent = jnp.einsum('bnc,c->bn', q, w_conv1)
        agent_attn = jax.nn.softmax(jnp.einsum('bn,bnc->bc', agent * scale, k), axis=-1)
        agent_v = jax.nn.softmax(jnp.einsum('bc,bnc->bn', agent_attn, v), axis=-1)
        agent_v = jnp.einsum('bn,bnc->bc', agent_v, v)
        agent_tok = jax.nn.softmax(agent[:, :, None], axis=-1)
        return agent_tok * agent_v[:, None, :]

    def _L0_xattn_ref(query, key, value, cell_mask, seq_mask, W_k, b_k, W_o, b_o):
        import jax, jax.numpy as jnp
        import numpy as np
        k_proj = jnp.einsum('bkd,qd->bkq', key, W_k) + b_k
        scores = jnp.einsum('bqd,bkd->bqk', query, k_proj)
        scores = scores + jnp.log(cell_mask) + jnp.log(seq_mask)[:, None, :]
        p_attn = jax.nn.softmax(scores, axis=-1)
        x = jnp.einsum('bqk,bkd->bqd', p_attn, value)
        return jnp.einsum('bqd,od->bqo', x, W_o) + b_o

    def _L0_ffn_ref(token_inputs, Wg, Wq, Wk, Wv, Wo):
        import jax, jax.numpy as jnp
        import numpy as np
        CAPACITY_FACTOR = 0.5
        NUM_HEADS = 16
        B, N, D = token_inputs.shape
        C = int(N * CAPACITY_FACTOR)
        H = NUM_HEADS
        dh = D // H
        gate = jax.nn.sigmoid((token_inputs @ Wg)[..., 0])
        _, idx = jax.lax.top_k(gate, C)
        attn_in = jnp.take_along_axis(token_inputs, idx[..., None], axis=1)
        q = (attn_in @ Wq).reshape(B, C, H, dh)
        k = (attn_in @ Wk).reshape(B, C, H, dh)
        v = (attn_in @ Wv).reshape(B, C, H, dh)
        scores = jnp.einsum('bqhd,bkhd->bhqk', q, k) / jnp.sqrt(jnp.float32(dh))
        attn = jax.nn.softmax(scores, axis=-1)
        o = jnp.einsum('bhqk,bkhd->bqhd', attn, v).reshape(B, C, D) @ Wo
        gate_sel = jnp.take_along_axis(gate, idx, axis=1)
        out = jnp.zeros_like(token_inputs)
        out = out.at[jnp.arange(B)[:, None], idx].set(o * gate_sel[..., None])
        return out

    def _L1_attn_ref(hidden_states, Wq, bq, Wk, bk, Wv, bv, Wo, bo):
        import jax, jax.numpy as jnp
        import numpy as np
        EMBED_DIM = 256
        NUM_HEADS = 16
        HEAD_DIM = EMBED_DIM // NUM_HEADS
        WINDOW_SIZE = 32
        HALF_BAND = 2 * WINDOW_SIZE
        BAND = 2 * HALF_BAND + 1
        B, T, E = hidden_states.shape
        H, D = (NUM_HEADS, HEAD_DIM)
        S = T
        q = hidden_states @ Wq.T + bq
        k = hidden_states @ Wk.T + bk
        v = hidden_states @ Wv.T + bv
        q = q.reshape(B, T, H, D).transpose(0, 2, 1, 3)
        k = k.reshape(B, S, H, D).transpose(0, 2, 1, 3)
        v = v.reshape(B, S, H, D).transpose(0, 2, 1, 3)
        offsets = jnp.arange(-HALF_BAND, HALF_BAND + 1)
        idx = jnp.arange(T)[:, None] + offsets[None, :]
        valid = (idx >= 0) & (idx < S)
        idxc = jnp.clip(idx, 0, S - 1)
        kb = k[:, :, idxc, :]
        vb = v[:, :, idxc, :]
        scaling = jnp.sqrt(jnp.asarray(D, jnp.float32))
        scores = jnp.einsum('bhtd,bhtwd->bhtw', q, kb) / scaling
        scores = jnp.where(valid[None, None], scores, -jnp.inf)
        probs = jax.nn.softmax(scores, axis=-1)
        ctx = jnp.einsum('bhtw,bhtwd->bhtd', probs, vb)
        ctx = ctx.transpose(0, 2, 1, 3).reshape(B, T, H * D)
        attn_output = ctx @ Wo.T + bo
        return attn_output

    def _L1_xattn_ref(query, key, value, Wq, bq, Wk, bk, Wv, bv, Wo, bo):
        import jax, jax.numpy as jnp
        import numpy as np
        D = 256
        Q = jnp.einsum('bsd,de->bse', query, Wq) + bq
        K = jnp.einsum('bsd,de->bse', key, Wk) + bk
        V = jnp.einsum('bsd,de->bse', value, Wv) + bv
        scale = 1.0 / jnp.sqrt(jnp.asarray(D, Q.dtype))
        scores = jnp.einsum('bqd,bkd->bqk', Q, K) * scale
        attn = jax.nn.softmax(scores, axis=-1)
        out = jnp.einsum('bqk,bkd->bqd', attn, V)
        return jnp.einsum('bsd,de->bse', out, Wo) + bo

    def _L1_ffn_ref(x, w_int8, weight_scale, bias):
        import jax, jax.numpy as jnp
        import numpy as np
        EPS_RMS = 1e-06
        EPS_ACT = 1e-05

        def simple_rms_norm(x):
            ms = jnp.mean(jnp.square(x), axis=-1, keepdims=True)
            return x * jax.lax.rsqrt(ms + EPS_RMS)

        def activation_quant(x):
            absmax = jnp.max(jnp.abs(jax.lax.stop_gradient(x)), axis=-1, keepdims=True)
            scale = 127.0 / jnp.clip(absmax, EPS_ACT, None)
            q = jnp.clip(jnp.round(x * scale), -128.0, 127.0) / scale
            return x + jax.lax.stop_gradient(q - x)
        w_deq = w_int8.astype(jnp.float32) * (1.0 / weight_scale) * weight_scale ** 0 * weight_scale
        w_deq = w_int8.astype(jnp.float32) * weight_scale
        x_norm = simple_rms_norm(x)
        x_q = activation_quant(x_norm)
        return jnp.einsum('bsd,od->bso', x_q, w_deq) + bias
    x = _layernorm(x + _L0_attn_ref(x, L0_attn_w_qkv, L0_attn_w_conv1), axis=-1)
    x = _layernorm(x + _L0_xattn_ref(x, ctx_1024, ctx_1024, mask_BxSxS2_ff1, mask_BxS2_ff1, L0_xattn_W_k, L0_xattn_b_k, L0_xattn_W_o, L0_xattn_b_o), axis=-1)
    x = _layernorm(x + _L0_ffn_ref(x, L0_ffn_Wg, L0_ffn_Wq, L0_ffn_Wk, L0_ffn_Wv, L0_ffn_Wo), axis=-1)
    x = _layernorm(x + _L1_attn_ref(x, L1_attn_Wq, L1_attn_bq, L1_attn_Wk, L1_attn_bk, L1_attn_Wv, L1_attn_bv, L1_attn_Wo, L1_attn_bo), axis=-1)
    x = _layernorm(x + _L1_xattn_ref(x, ctx_1024, ctx_1024, L1_xattn_Wq, L1_xattn_bq, L1_xattn_Wk, L1_xattn_bk, L1_xattn_Wv, L1_xattn_bv, L1_xattn_Wo, L1_xattn_bo), axis=-1)
    x = _layernorm(x + _L1_ffn_ref(x, L1_ffn_w_int8, L1_ffn_weight_scale, L1_ffn_bias), axis=-1)
    return x

_drawn_inputs = setup_inputs


def setup_inputs(seed=0):
    import zlib

    import numpy as np

    out = dict(_drawn_inputs(seed))
    spreads = {'L0_xattn_b_k': (0.0, 2.0),
     'L0_xattn_b_o': (0.0, 0.1),
     'L1_xattn_bq': (0.0, 0.8),
     'L1_xattn_bk': (0.0, 2.0),
     'L1_xattn_bv': (0.0, 0.1),
     'L1_xattn_bo': (0.0, 0.1)}
    factors = {'L1_attn_Wq': 8.0,
     'L1_attn_bq': 37.195,
     'L1_attn_Wk': 8.0,
     'L1_attn_bk': 64.0,
     'L1_attn_bv': 6.194,
     'L1_attn_bo': 2.695,
     'L1_xattn_Wq': 8.0,
     'L1_xattn_Wk': 8.0,
     'L1_ffn_bias': 64.0}
    for name, (base, spread) in spreads.items():
        noise = np.random.default_rng([zlib.crc32(name.encode()), seed]).standard_normal(out[name].shape)
        drawn = base * np.exp(spread * noise) if base else spread * noise
        out[name] = jnp.asarray(drawn.astype(out[name].dtype))
    for name, factor in factors.items():
        out[name] = (out[name] * factor).astype(out[name].dtype)
    return out
```

```python
import numpy as np
from contextlib import ExitStack

import concourse.bass as bass
from concourse import mybir

LAST_LAYER = 6

F32 = mybir.dt.float32
BF16 = mybir.dt.bfloat16
I32 = mybir.dt.int32
ALU = mybir.AluOpType
ACT = mybir.ActivationFunctionType
AX = mybir.AxisListType.X

B, S, D, S2 = 32, 100, 256, 361
H, DH = 16, 16
P = 128
NC = D // P
G = 4
NI = B // G
NB = 2
T = NB * S
S2C = 3
CAP = S // 2
SLOT = 64
BAND = 64
NEDGE = S - 1 - BAND
NM = 2 * NEDGE
ROWS = P // 32
NEG = -1.0e30
TINY = 2.0 ** -63
ROUND = 1.5 * 2.0 ** 23
LN_EPS, RMS_EPS, ACT_EPS = 1e-5, 1e-6, 1e-5


def place(h):
    c, g, j = h // 8, (h % 8) // 2, h % 2
    return c, g, j, 4 * g + 2 * c + j


class Queue:

    def __init__(self, name, sem):
        self.name, self.sem = name, sem
        self.restart()

    def restart(self):
        self.steps, self.count, self.seen = [], 0, {}

    def wait(self, *events):
        for sem, value in events:
            if self.seen.get(id(sem), 0) < value:
                self.seen[id(sem)] = value
                self.steps.append(lambda e, i, sem=sem, value=value: e.wait_ge(sem, value))

    def put(self, make, after=(), signal=True):
        self.wait(*[ev for ev in after if ev is not None])
        if not signal:
            self.steps.append(lambda e, i: make(e))
            return None
        self.count += 1
        self.steps.append(lambda e, i: make(e).then_inc(self.sem, 1))
        return (self.sem, self.count)

    def now(self, make):
        self.steps.append(make)

    def run(self, e, i=None):
        for step in self.steps:
            step(e, i)


class Bank:

    def __init__(self, ap):
        self.ap, self.bf, self.free = ap, ap.bitcast(BF16), None


def program(nc, ins, out):
    ctx = ExitStack()
    with ctx:
        def sb(name, shape, dt=F32):
            return ctx.enter_context(nc.sbuf_tensor(name, list(shape), dt))

        def sem(name):
            return ctx.enter_context(nc.semaphore(name))

        W = {n: sb(n, [P, NC, D]) for n in WEIGHTS}
        rows = {n: sb(n + "_r", [P, D]) for n in ROWVECS}
        cols = {n: sb(n + "_c", [P, NC]) for n in COLVECS}
        w8 = sb("w8", [P, NC, D], BF16)
        wscale = sb("wscale", [P, 1])
        qscale = sb("qscale", [P, 1])
        ident = sb("ident", [P, P])
        ident_b = sb("ident_b", [P, P], BF16)
        ones = sb("ones", [P, P])
        before = sb("before", [S, S])
        slots = sb("slots", [S, SLOT])
        parity = sb("parity", [P, 2])
        pick_batch = sb("pick_batch", [G, G, S])
        edge_key = sb("edge_key", [NM, S], BF16)
        edge_mask = sb("edge_mask", [NM, S], BF16)
        shift1_w = sb("shift1_w", [2 * H + NM, H, S], BF16)
        shift1_x = sb("shift1_x", [2 * H + NM, S], BF16)
        shift0_w = sb("shift0_w", [2 * H + 1, H, SLOT], BF16)
        agent_w = sb("agent_w", [P, D])
        bo1 = sb("bo1", [P, D])
        wqk = sb("wqk", [P, NC, D])
        bqk = sb("bqk", [P, NC])
        wqbk = sb("wqbk", [P, D])
        bqbk = sb("bqbk", [P, 1])
        wvo = sb("wvo", [P, NC, D])
        bvo = sb("bvo", [P, D])
        bkp = sb("bkp", [P, 2, NC])

        xin = sb("xin", [S, G, D])
        ag = sb("ag", [S, G])
        tok = sb("tok", [S, G])
        tokd = sb("tokd", [S, G])
        toke = sb("toke", [S, G])
        tokr = sb("tokr", [S, G])
        ajunk = sb("ajunk", [S, D])
        yT = sb("yT", [P, NC, G])
        arow = sb("arow", [G, D])
        arow2 = sb("arow2", [G, D])
        astat = sb("astat", [G, 8])
        aT = sb("aT", [P, NC, G])
        zT = sb("zT", [P, NC, G])
        xinT = sb("xinT", [P, NC, G * S])
        lcol = sb("lcol", [S, G])
        lrow = sb("lrow", [G, S])
        lrow2 = sb("lrow2", [G, S])
        acol = sb("acol", [S, G])
        avT = sb("avT", [P, NC, G])
        agent_v = sb("agent_v", [G, D])

        class Stream:

            def __init__(s, n):
                s.n = n
                s.x = sb(f"x{n}", [S, NB, D])
                s.xb = sb(f"xb{n}", [S, NB, D])
                s.r = sb(f"r{n}", [S, NB, D])
                s.xT = sb(f"xT{n}", [P, NC, T])
                s.aT = sb(f"aT{n}", [P, NC, T])
                s.qT = sb(f"qT{n}", [P, NC, T])
                s.kT = sb(f"kT{n}", [P, 2, NC, T])
                s.v = sb(f"v{n}", [S, NB, H, DH + 1])
                s.E = sb(f"E{n}", [P, H, S])
                s.o = sb(f"o{n}", [P, NB, D])
                s.ctx = sb(f"ctx{n}", [P, NB, S2C, D])
                s.ctxT = sb(f"ctxT{n}", [P, NB, NC, S2])
                s.cell = sb(f"cell{n}", [S, NB, S2])
                s.seq = sb(f"seq{n}", [S, NB, S2])
                s.lmask = sb(f"lmask{n}", [S, NB, S2])
                s.zero = sb(f"zero{n}", [S, NB, S2])
                s.sm = sb(f"sm{n}", [S, NB, S2])
                s.p = sb(f"p{n}", [S, NB, S2C * P])
                s.pT = sb(f"pT{n}", [P, S2C, S])
                s.prod = sb(f"prod{n}", [S, NB, D])
                s.qb = sb(f"qb{n}", [S, NB])
                s.bn = sb(f"bn{n}", [S, NB, 6])
                s.mv = sb(f"mv{n}", [S, NB, 2])
                s.ve = sb(f"ve{n}", [S, NB])
                s.rstd = sb(f"rstd{n}", [S, NB])
                s.mx = sb(f"mx{n}", [P, H])
                s.mx2 = sb(f"mx2{n}", [P, NB])
                s.nb = sb(f"nb{n}", [S, NB])
                s.sum = sb(f"sum{n}", [S, NB])
                s.rsum = sb(f"rsum{n}", [S, NB])
                s.hl = sb(f"hl{n}", [P, 2 * H], BF16)
                s.rden = sb(f"rden{n}", [P, H])
                s.z = sb(f"z{n}", [S, NB])
                s.ez = sb(f"ez{n}", [S, NB])
                s.gp = sb(f"gp{n}", [S, NB])
                s.gate = sb(f"gate{n}", [S, NB])
                s.dg = sb(f"dg{n}", [S, NB, S])
                s.tie = sb(f"tie{n}", [S, S])
                s.above = sb(f"above{n}", [S, S])
                s.rank = sb(f"rank{n}", [S, NB])
                s.sel = sb(f"sel{n}", [S, NB, SLOT])
                s.selT = sb(f"selT{n}", [P, S])
                s.v0 = sb(f"v0{n}", [P, H, DH + 1])
                s.shift0_x = sb(f"shift0_x{n}", [2 * H + 1, P], BF16)
                s.shift1_x = sb(f"shift1_x{n}", [2 * H + NM, S], BF16)
                s.ms = sb(f"ms{n}", [S, NB])
                s.rms = sb(f"rms{n}", [S, NB])
                s.am = sb(f"am{n}", [S, NB])
                s.am2 = sb(f"am2{n}", [S, NB])
                s.sc = sb(f"sc{n}", [S, NB])
                s.ra = sb(f"ra{n}", [S, NB])
                s.os = sb(f"os{n}", [S, NB])
                s.yq = sb(f"yq{n}", [S, NB, D], BF16)
                s.yT = sb(f"yT{n}", [P, NC, T], BF16)
                s.out = sb(f"out{n}", [S, NB, D])

        streams = []
        for n in range(G // NB):
            s = Stream(n)
            s.sT, s.q0, s.o0T = s.xT[:, :, 0:P], s.qT[:, :, 0:P], s.aT[:, :, 0:P]
            s.k0 = s.kT[:, :, :, 0:P]
            s.E0 = s.E[:, :, 0:SLOT]
            s.o0, s.w0 = s.o[:, 0, :], s.o[:, 1, :]
            s.y = s.prod
            streams.append(s)

        w8_i = streams[0].E[:, 0:6, :].rearrange("p h s -> p (h s)")[:, 0:NC * D].bitcast(I32)
        psum = ctx.enter_context(nc.psum_tensor("psum", [P, 8, 512], F32))
        banks = [Bank(psum[:, k, :]) for k in range(8)]

        PE, VE, AC, PO = (Queue(n, sem("s_" + n)) for n in ("tensor", "vector", "scalar", "gpsimd"))
        SY = Queue("sync", None)
        engines = [PE, VE, AC, PO]
        s_const = sem("s_const")
        s_xin = sem("s_xin")
        s_ctx = [sem(f"s_ctx{n}") for n in range(G // NB)]
        s_mask = [sem(f"s_mask{n}") for n in range(G // NB)]
        s_store = [sem(f"s_store{n}") for n in range(G // NB)]
        s_arrive = sem("s_arrive")
        s_go = {n: sem("s_go_" + n) for n in ("tensor", "vector", "scalar", "sync")}

        def mm(dst, w, x, start=True, stop=True, after=(), signal=False, shared=False):
            return PE.put(lambda e: e.matmul(dst, w, x, start=start, stop=stop, skip_group_check=shared),
                          after, signal)

        def tr(dst, src, idn, after=(), signal=False):
            return PE.put(lambda e: e.transpose(dst, src, idn), after, signal)

        def act(dst, src, fn=ACT.Copy, after=(), **kw):
            return AC.put(lambda e: e.activation(dst, src, fn, **kw), after)

        def copy(q, dst, src, after=()):
            if q is AC:
                return act(dst, src, after=after)
            return q.put(lambda e: e.tensor_copy(dst, src), after)

        def ts(q, dst, src, s1, op0, s2=None, op1=None, after=()):
            if op1 is None:
                return q.put(lambda e: e.tensor_scalar(dst, src, s1, None, op0), after)
            return q.put(lambda e: e.tensor_scalar(dst, src, s1, s2, op0, op1), after)

        def tt(q, dst, a, b, op, after=()):
            return q.put(lambda e: e.tensor_tensor(dst, a, b, op), after)

        def stt(dst, a, s1, b, op0, op1, after=(), **kw):
            return VE.put(lambda e: e.scalar_tensor_tensor(dst, a, s1, b, op0, op1, **kw), after)

        def reduce(q, dst, src, op, after=()):
            return q.put(lambda e: e.tensor_reduce(dst, src, AX, op), after)

        def recip(dst, src, after=()):
            return VE.put(lambda e: e.reciprocal(dst, src), after)

        def transpose_tokens(src, dst, bank, ready):
            for c in range(NC):
                for b in range(NB):
                    last = tr(bank.ap[:, (c * NB + b) * S:(c * NB + b + 1) * S],
                              src[:, b, c * P:(c + 1) * P], ident[0:S, 0:S],
                              after=(ready, bank.free), signal=(c, b) == (NC - 1, NB - 1))
            bank.free = act(dst[:, :, :].rearrange("p c t -> p (c t)"), bank.ap[:, 0:NC * T], after=(last,))
            return bank.free

        def project(w, xT, bank, n, at=0, after=()):
            for e in range(NC):
                for c in range(NC):
                    last = mm(bank.ap[:, at + e * n:at + (e + 1) * n], w[:, c, e * P:(e + 1) * P], xT[:, c, 0:n],
                              start=c == 0, stop=c == NC - 1, after=(*after, bank.free),
                              signal=(e, c) == (NC - 1, NC - 1))
            return last

        def project_tokens(xT, w, bank, after=()):
            for b in range(NB):
                for c in range(NC):
                    last = mm(bank.ap[0:S, b * D:(b + 1) * D], xT[:, c, b * S:(b + 1) * S], w[:, c, :],
                              start=c == 0, stop=c == NC - 1, after=(*after, bank.free),
                              signal=(b, c) == (NB - 1, NC - 1))
            return last

        def layernorm(s, dst, ready, after=()):
            for b in range(NB):
                st = VE.put(lambda e, b=b: e.bn_stats(s.bn[:, b, :], s.r[:, b, :]), after=(ready[b],))
                ag_ = VE.put(lambda e, b=b: e.bn_aggr(s.mv[:, b, :], s.bn[:, b, :]), after=(st,))
            ev = ts(PO, s.ve[:, :], s.mv[:, :, 1], LN_EPS, ALU.add, after=(ag_,))
            ev = tt(PO, s.rstd[:, :], s.ve[:, :], minus_half[0:S, 0:NB], ALU.pow, after=(ev,))
            for b in range(NB):
                last = ts(VE, dst[:, b, :], s.r[:, b, :], s.mv[:, b, 0:1], ALU.subtract,
                          s.rstd[:, b:b + 1], ALU.mult, after=(ev, *after))
            return last

        def add_row(s, row, ready):
            return tt(PO, s.xb[:, :, :], s.x[:, :, :], row[0:S, :].unsqueeze(1).to_broadcast([S, NB, D]),
                      ALU.add, after=(ready,))

        def const_score(s, row, ready):
            ev = tt(PO, s.prod[:, :, :], s.x[:, :, :], row[0:S, :].unsqueeze(1).to_broadcast([S, NB, D]),
                    ALU.mult, after=(ready,))
            for b in range(NB):
                last = act(s.prod[:, b, :], s.prod[:, b, :], after=(ev,), accum_out=s.qb[:, b:b + 1])
            s.prod_used = last
            return last

        minus_half = sb("minus_half", [P, NB])

        def agent(loaded, kept):
            bank = banks[3]
            AC.now(loaded)
            VE.now(loaded)
            PE.now(loaded)
            for b in range(G):
                ev = stt(ajunk[:, :], xin[:, b, :], 1.0, agent_w[0:S, :], ALU.mult, ALU.mult,
                         after=(VE_last(),), accum_out=ag[:, b:b + 1])
            e1 = tt(VE, tokd[:, :], ag[:, :], ag[:, :], ALU.subtract, after=(ev,))
            e2 = act(toke[:, :], tokd[:, :], ACT.Exp, after=(e1,))
            yield
            for c in range(NC):
                for b in range(G):
                    last = mm(bank.ap[:, c * G + b:c * G + b + 1], xin[:, b, c * P:(c + 1) * P], ag[:, b:b + 1],
                              after=(ev, bank.free), signal=(c, b) == (NC - 1, G - 1))
            bank.free = ts(VE, yT[:, :, :].rearrange("p c b -> p (c b)"), bank.ap[:, 0:NC * G],
                           float(D) ** -0.5, ALU.mult, after=(last,))
            e1 = recip(tokr[:, :], toke[:, :], after=(e2,))
            tok_ready = tt(VE, tok[:, :], toke[:, :], tokr[:, :], ALU.mult, after=(e1, *kept))
            yield
            for c in range(NC):
                last = mm(bank.ap[0:G, 0:D], yT[:, c, :], W["w_k0"][:, c, :], start=c == 0, stop=c == NC - 1,
                          after=(bank.free,), signal=c == NC - 1)
            yield
            e1 = reduce(VE, astat[:, 0:1], bank.ap[0:G, 0:D], ALU.max, after=(last,))
            e1 = ts(VE, astat[:, 1:2], astat[:, 0:1], -1.0, ALU.mult, after=(e1,))
            bank.free = e1 = act(arow[:, :], bank.ap[0:G, 0:D], ACT.Exp, after=(e1,), bias=astat[:, 1:2],
                                 accum_out=astat[:, 2:3])
            yield
            e1 = recip(astat[:, 3:4], astat[:, 2:3], after=(e1,))
            e1 = ts(VE, arow2[:, :], arow[:, :], astat[:, 3:4], ALU.mult, after=(e1,))
            for c in range(NC):
                last = tr(bank.ap[:, c * G:(c + 1) * G], arow2[:, c * P:(c + 1) * P], ident[0:G, 0:G],
                          after=(e1, bank.free), signal=c == NC - 1)
            bank.free = copy(VE, aT[:, :, :].rearrange("p c b -> p (c b)"), bank.ap[:, 0:NC * G], after=(last,))
            yield
            for e in range(NC):
                for c in range(NC):
                    last = mm(bank.ap[:, e * G:(e + 1) * G], W["w_v0"][:, c, e * P:(e + 1) * P], aT[:, c, :],
                              start=c == 0, stop=c == NC - 1, after=(bank.free,), signal=(e, c) == (NC - 1, NC - 1))
            bank.free = ez = copy(VE, zT[:, :, :].rearrange("p c b -> p (c b)"), bank.ap[:, 0:NC * G], after=(last,))
            yield
            for c in range(NC):
                for b in range(G):
                    last = tr(bank.ap[:, b * S:(b + 1) * S], xin[:, b, c * P:(c + 1) * P], ident[0:S, 0:S],
                              after=(bank.free,), signal=b == G - 1)
                bank.free = act(xinT[:, c, :], bank.ap[:, 0:G * S], after=(last,))
                yield
            for b in range(G):
                for c in range(NC):
                    last = mm(bank.ap[0:S, b:b + 1], xinT[:, c, b * S:(b + 1) * S], zT[:, c, b:b + 1],
                              start=c == 0, stop=c == NC - 1, after=(ez, bank.free), signal=(b, c) == (G - 1, NC - 1))
            bank.free = e1 = copy(VE, lcol[:, :], bank.ap[0:S, 0:G], after=(last,))
            yield
            last = tr(bank.ap[0:G, 0:S], lcol[:, :], ident[0:S, 0:S], after=(e1,), signal=True)
            e1 = reduce(VE, astat[:, 4:5], bank.ap[0:G, 0:S], ALU.max, after=(last,))
            e1 = ts(VE, astat[:, 5:6], astat[:, 4:5], -1.0, ALU.mult, after=(e1,))
            bank.free = e1 = act(lrow[:, :], bank.ap[0:G, 0:S], ACT.Exp, after=(e1,), bias=astat[:, 5:6],
                                 accum_out=astat[:, 6:7])
            yield
            e1 = recip(astat[:, 7:8], astat[:, 6:7], after=(e1,))
            e1 = ts(VE, lrow2[:, :], lrow[:, :], astat[:, 7:8], ALU.mult, after=(e1,))
            last = tr(bank.ap[0:S, 0:G], lrow2[:, :], ident[0:G, 0:G], after=(e1, bank.free), signal=True)
            bank.free = e1 = copy(VE, acol[:, :], bank.ap[0:S, 0:G], after=(last,))
            yield
            for c in range(NC):
                for b in range(G):
                    last = mm(bank.ap[:, c * G + b:c * G + b + 1], xin[:, b, c * P:(c + 1) * P], acol[:, b:b + 1],
                              after=(e1, bank.free), signal=(c, b) == (NC - 1, G - 1))
            bank.free = copy(VE, avT[:, :, :].rearrange("p c b -> p (c b)"), bank.ap[:, 0:NC * G], after=(last,))
            yield
            for c in range(NC):
                last = mm(bank.ap[0:G, 0:D], avT[:, c, :], W["w_v0T"][:, c, :], start=c == 0, stop=c == NC - 1,
                          after=(bank.free,), signal=c == NC - 1)
            bank.free = copy(VE, agent_v[:, :], bank.ap[0:G, 0:D], after=(last, *kept))
            yield

        def VE_last():
            return (VE.sem, VE.count) if VE.count else None

        def sub_agent(s, bk):
            ready = [None] * NB
            for b in range(NB):
                last = mm(bk[0].ap[0:S, b * D:(b + 1) * D], pick_batch[:, NB * s.n + b, :], agent_v[:, :],
                          after=(bk[0].free,), signal=b == NB - 1)
            for b in range(NB):
                n = NB * s.n + b
                ready[b] = stt(s.r[:, b, :], bk[0].ap[0:S, b * D:(b + 1) * D], tok[:, n:n + 1], xin[:, n, :],
                               ALU.mult, ALU.add, after=(last,))
            bk[0].free = ready[-1]
            s.agent_used = (last, ready[-1])
            yield
            s.x_ready = layernorm(s, s.x, ready)

        def log_masks(s):
            e1 = tt(PO, s.cell[:, :, :], s.cell[:, :, :], s.seq[:, :, :], ALU.mult)
            e2 = ts(PO, s.zero[:, :, :], s.cell[:, :, :], 0.0, ALU.is_equal, 3.0 * NEG, ALU.mult, after=(e1,))
            e1 = ts(PO, s.sm[:, :, :], s.cell[:, :, :], TINY, ALU.max, after=(e1,))
            e1 = act(s.sm[:, :, :], s.sm[:, :, :], ACT.Ln, after=(e1,))
            s.mask_ready = tt(PO, s.lmask[:, :, :], s.sm[:, :, :], s.zero[:, :, :], ALU.add, after=(e1, e2))

        def cross(s, bk, wq, bq_cols, row_bk, add_bk, wo, row_o, masked):
            e_xT = transpose_tokens(s.x, s.xT, bk[0], s.x_ready)
            e_xb = add_row(s, row_o, s.x_ready)
            e_qb = const_score(s, row_bk, s.x_ready)
            if add_bk is not None:
                e_qb = ts(PO, s.qb[:, :], s.qb[:, :], add_bk[0:S, :], ALU.add, after=(e_qb,))
            yield
            last = project(wq, s.xT, bk[1], T, after=(e_xT,))
            for e in range(NC):
                if bq_cols is None:
                    ev = act(s.qT[:, e, :], bk[1].ap[:, e * T:(e + 1) * T], after=(last,))
                else:
                    ev = act(s.qT[:, e, :], bk[1].ap[:, e * T:(e + 1) * T], ACT.Identity, after=(last,),
                             bias=bq_cols[:, e:e + 1])
            bk[1].free = e_q = ev
            yield
            e_p = [None] * NB
            for b in range(NB):
                k = bk[b]
                for c in range(NC):
                    last = mm(k.ap[0:S, 0:S2], s.qT[:, c, b * S:(b + 1) * S], s.ctxT[:, b, c, :],
                              start=c == 0, stop=c == NC - 1, after=(e_q, k.free), signal=c == NC - 1)
                if masked:
                    ev = VE.put(lambda e, b=b, k=k: e.tensor_tensor_reduce(
                        out=s.sm[:, b, :], in0=k.ap[0:S, 0:S2], in1=s.lmask[:, b, :], scale=1.0, scalar=3.0 * NEG,
                        op0=ALU.add, op1=ALU.max, accum_out=s.mx2[0:S, b:b + 1]), after=(last, s.mask_ready))
                    k.free = ev
                    src = s.sm[:, b, :]
                else:
                    ev = reduce(VE, s.mx2[0:S, b:b + 1], k.ap[0:S, 0:S2], ALU.max, after=(last,))
                    src = k.ap[0:S, 0:S2]
                ev = stt(s.nb[:, b:b + 1], s.mx2[0:S, b:b + 1], s.qb[:, b:b + 1], s.qb[:, b:b + 1],
                         ALU.add, ALU.subtract, after=(ev, e_qb), reverse1=True)
                e_p[b] = act(s.p[:, b, 0:S2], src, ACT.Exp, after=(ev,), bias=s.nb[:, b:b + 1],
                             accum_out=s.sum[:, b:b + 1])
                if not masked:
                    k.free = e_p[b]
            e_r = recip(s.rsum[:, :], s.sum[:, :], after=(e_p[-1],))
            yield
            for b in range(NB):
                k = bk[2]
                for j in range(S2C):
                    last = tr(k.ap[:, j * S:(j + 1) * S], s.p[:, b, j * P:(j + 1) * P], ident[0:S, 0:S],
                              after=(e_p[b], k.free), signal=j == S2C - 1)
                k.free = e_pT = copy((VE, AC)[b], s.pT[:, :, :].rearrange("p j t -> p (j t)"), k.ap[:, 0:S2C * S],
                                     after=(last,))
                yield
                k = bk[3]
                for c in range(NC):
                    for j in range(S2C):
                        last = mm(k.ap[:, c * S:(c + 1) * S], s.ctx[:, b, j, c * P:(c + 1) * P], s.pT[:, j, :],
                                  start=j == 0, stop=j == S2C - 1, after=(e_pT, k.free),
                                  signal=(c, j) == (NC - 1, S2C - 1))
                k.free = e_a = copy((AC, VE)[b], s.aT[:, :, b * S:(b + 1) * S],
                                    k.ap[:, 0:NC * S].rearrange("p (c t) -> p c t", c=NC), after=(last,))
                if b == 0:
                    e_a0 = e_a
            s.ctx_used = last
            yield
            last = project_tokens(s.aT, wo, bk[0], after=(e_a0, e_a))
            ready = [stt(s.r[:, b, :], bk[0].ap[0:S, b * D:(b + 1) * D], s.rsum[:, b:b + 1], s.xb[:, b, :],
                         ALU.mult, ALU.add, after=(last, e_r, e_xb)) for b in range(NB)]
            bk[0].free = ready[-1]
            yield
            s.x_ready = layernorm(s, s.x, ready)

        def split_max(s, n, ready, bank, dst):
            ev = ts(VE, s.hl[0:n, 0:H], s.mx[0:n, :], -1.0, ALU.mult, after=(ready,))
            ev = stt(s.hl[0:n, H:2 * H], s.mx[0:n, :], -1.0, s.hl[0:n, 0:H], ALU.mult, ALU.subtract, after=(ev,))
            last = tr(bank.bf[0:2 * H, 0:n], s.hl[0:n, :], ident_b[0:n, 0:n], after=(ev, bank.free), signal=True)
            bank.free = copy(VE, dst[0:2 * H, 0:n], bank.bf[0:2 * H, 0:n], after=(last,))
            return bank.free

        def sub_select(s, bk):
            for b in range(NB):
                ev = stt(s.prod[:, b, :], s.x[:, b, :], 1.0, rows["f_wg"][0:S, :], ALU.mult, ALU.mult,
                         after=(s.x_ready, s.prod_used), accum_out=s.z[:, b:b + 1])
            ev = act(s.ez[:, :], s.z[:, :], ACT.Exp, after=(ev,), scale=-1.0)
            ev = ts(VE, s.gp[:, :], s.ez[:, :], 1.0, ALU.add, after=(ev,))
            e_g = recip(s.gate[:, :], s.gp[:, :], after=(ev,))
            for b in range(NB):
                e_d = ts(VE, s.dg[:, b, :], ident[0:S, 0:S], s.gate[:, b:b + 1], ALU.mult, after=(e_g,))
            yield
            last = mm(bk[0].ap[0:S, 0:T], ones[0:S, 0:S], s.dg[:, :, :].rearrange("p b t -> p (b t)"),
                      after=(e_d, bk[0].free), signal=True)
            for b in range(NB):
                gates = bk[0].ap[0:S, b * S:(b + 1) * S]
                ev = stt(s.tie[:, :], gates, s.gate[:, b:b + 1], before[:, :], ALU.is_equal, ALU.mult,
                         after=(last, VE_last()))
                ev = stt(s.above[:, :], gates, s.gate[:, b:b + 1], s.tie[:, :], ALU.is_gt, ALU.add,
                         after=(ev,), accum_out=s.rank[:, b:b + 1])
            bk[0].free = ev
            for b in range(NB):
                e_s = ts(VE, s.sel[:, b, :], slots[:, :], s.rank[:, b:b + 1], ALU.is_equal, after=(ev,))
            yield
            tr(bk[1].ap[:, 0:S], s.sel[:, :, :].rearrange("p b m -> p (b m)"), ident[0:S, 0:S],
               after=(e_s, bk[1].free))
            for c in range(NC):
                for b in range(NB):
                    last = mm(bk[1].ap[:, 128 + c * P + b * SLOT:128 + c * P + (b + 1) * SLOT],
                              s.x[:, b, c * P:(c + 1) * P], s.sel[:, b, :], after=(bk[1].free,),
                              signal=(c, b) == (NC - 1, NB - 1))
            e_sT = act(s.sT[:, :, :], bk[1].ap[:, 128:128 + NC * P].rearrange("p (c m) -> p c m", c=NC), after=(last,))
            e_selT = act(s.selT[:, :], bk[1].ap[:, 0:S], after=(last,))
            bk[1].free = e_selT
            yield
            last = project(W["f_q"], s.sT, bk[2], P, after=(e_sT,))
            e_q = act(s.q0[:, :, :], bk[2].ap[:, 0:NC * P].rearrange("p (c m) -> p c m", c=NC), after=(last,))
            bk[2].free = e_q
            last = project(W["f_k"], s.sT, bk[3], P)
            for j in range(2):
                e_k = ts(VE, s.k0[:, j, :, :], bk[3].ap[:, 0:NC * P].rearrange("p (c m) -> p c m", c=NC),
                         parity[:, j:j + 1], ALU.mult, after=(last,))
            bk[3].free = e_k
            for c in range(NC):
                last = mm(bk[0].ap[:, 0:D], s.sT[:, c, :], W["f_v"][:, c, :], start=c == 0, stop=c == NC - 1,
                          after=(bk[0].free,), signal=c == NC - 1)
            bk[0].free = e_v = act(s.v0[:, :, 0:DH], bk[0].ap[:, 0:D].rearrange("p (h d) -> p h d", h=H),
                                   after=(last,))
            yield
            last = [None] * ROWS
            for c in range(NC):
                for j in range(2):
                    for b in range(NB):
                        for g in range(ROWS):
                            r, m = slice(32 * g, 32 * g + 32), slice(b * SLOT, (b + 1) * SLOT)
                            at = (2 * c + j) * CAP
                            last[g] = mm(bk[g].ap[m, at:at + CAP], s.q0[r, c, m],
                                         s.k0[r, j, c, b * SLOT:b * SLOT + CAP], after=(e_q, e_k, bk[g].free),
                                         signal=(c, j, b) == (NC - 1, 1, NB - 1))
            for g in range(0, ROWS, 2):
                k0 = 4 * s.n + g
                ev = reduce(VE, s.mx[:, 4 * g:4 * g + 8].rearrange("p (g q) -> p g q", g=2),
                            psum[:, k0:k0 + 2, 0:4 * CAP].rearrange("p g (q k) -> p g q k", q=4),
                            ALU.max, after=(last[g], last[g + 1]))
                bk[g].free = bk[g + 1].free = ev
            yield
            e_sh = split_max(s, P, ev, bk[3], s.shift0_x)
            yield
            for c in range(NC):
                for j in range(2):
                    for b in range(NB):
                        for g in range(ROWS):
                            r, m = slice(32 * g, 32 * g + 32), slice(b * SLOT, (b + 1) * SLOT)
                            at = (2 * c + j) * SLOT
                            mm(bk[g].ap[m, at:at + SLOT], s.k0[r, j, c, m], s.q0[r, c, m],
                               start=(c, j) == (0, 0), stop=False, after=(bk[g].free,), shared=True)
            for g in range(ROWS):
                for q in range(4):
                    for b in range(NB):
                        m = slice(b * SLOT, (b + 1) * SLOT)
                        last[g] = mm(bk[g].ap[m, q * SLOT:(q + 1) * SLOT], shift0_w[:, 4 * g + q, :],
                                     s.shift0_x[:, m], start=False, stop=True, after=(e_sh,), shared=True,
                                     signal=(q, b) == (3, NB - 1))
            for g in range(ROWS):
                e_E = act(s.E0[:, 4 * g:4 * g + 4, :], bk[g].ap[:, 0:4 * SLOT].rearrange("p (q m) -> p q m", q=4),
                          ACT.Exp, after=(last[g],), scale=float(DH) ** -0.5)
                bk[g].free = e_E
            yield
            for b in range(NB):
                m = slice(b * SLOT, (b + 1) * SLOT)
                for h in range(H):
                    last = mm(bk[0].ap[m, h * (DH + 1):(h + 1) * (DH + 1)], s.E0[m, place(h)[3], :], s.v0[m, h, :],
                              after=(e_E, e_v), signal=(b, h) == (NB - 1, H - 1))
            heads = bk[0].ap[:, 0:H * (DH + 1)].rearrange("p (h d) -> p h d", h=H)
            ev = recip(s.rden[:, :], heads[:, :, DH], after=(last,))
            ev = tt(VE, s.o0[:, :].rearrange("p (h d) -> p h d", h=H), heads[:, :, 0:DH],
                    s.rden[:, :].unsqueeze(2).to_broadcast([P, H, DH]), ALU.mult, after=(ev,))
            bk[0].free = ev
            yield
            for c in range(NC):
                last = tr(bk[1].ap[:, c * P:(c + 1) * P], s.o0[:, c * P:(c + 1) * P], ident[:, :],
                          after=(ev, bk[1].free), signal=c == NC - 1)
            bk[1].free = ev = act(s.o0T[:, :, :], bk[1].ap[:, 0:NC * P].rearrange("p (c m) -> p c m", c=NC), after=(last,))
            yield
            for c in range(NC):
                last = mm(bk[2].ap[:, 0:D], s.o0T[:, c, :], W["f_o"][:, c, :], start=c == 0, stop=c == NC - 1,
                          after=(ev, bk[2].free), signal=c == NC - 1)
            bk[2].free = ev = act(s.w0[:, :], bk[2].ap[:, 0:D], after=(last,))
            yield
            ready = [None] * NB
            for b in range(NB):
                k = bk[(3, 0)[b]]
                m = slice(b * SLOT, (b + 1) * SLOT)
                last = mm(k.ap[0:S, 0:D], s.selT[m, :], s.w0[m, :], after=(ev, e_selT, k.free), signal=True)
                k.free = ready[b] = stt(s.r[:, b, :], k.ap[0:S, 0:D], s.gate[:, b:b + 1], s.x[:, b, :],
                                        ALU.mult, ALU.add, after=(last,))
            yield
            s.x_ready = layernorm(s, s.x, ready)

        def sub_local(s, bk):
            e_xT = transpose_tokens(s.x, s.xT, bk[0], s.x_ready)
            e_xb = add_row(s, bo1, s.x_ready)
            yield
            last = project(W["a_q"], s.xT, bk[1], T, after=(e_xT,))
            for e in range(NC):
                e_q = act(s.qT[:, e, :], bk[1].ap[:, e * T:(e + 1) * T], ACT.Identity, after=(last,),
                          bias=cols["a_bq"][:, e:e + 1])
            bk[1].free = e_q
            last = project(W["a_k"], s.xT, bk[2], T)
            for j in range(2):
                for e in range(NC):
                    e_k = ts(VE, s.kT[:, j, e, :], bk[2].ap[:, e * T:(e + 1) * T], parity[:, j:j + 1], ALU.mult,
                             bkp[:, j, e:e + 1], ALU.add, after=(last,))
            bk[2].free = e_k
            last = project_tokens(s.xT, W["a_v"], bk[3])
            bk[3].free = e_v = act(s.v[:, :, :, 0:DH],
                                   bk[3].ap[0:S, 0:NB * D].rearrange("p (b h d) -> p b h d", b=NB, h=H), after=(last,))
            yield
            for b in range(NB):
                t = slice(b * S, (b + 1) * S)
                last = [None] * ROWS
                for c in range(NC):
                    for j in range(2):
                        for g in range(ROWS):
                            r = slice(32 * g, 32 * g + 32)
                            at = (2 * c + j) * S
                            mm(bk[g].ap[0:S, at:at + S], s.qT[r, c, t], s.kT[r, j, c, t],
                               start=(c, j) == (0, 0), stop=False, after=(e_q, e_k, bk[g].free), shared=True)
                for g in range(ROWS):
                    last[g] = mm(bk[g].ap[0:S, 0:4 * S], edge_key[:, :],
                                 edge_mask[:, :].unsqueeze(1).to_broadcast([NM, 4, S]), start=False, stop=True,
                                 shared=True, signal=True)
                for g in range(ROWS):
                    ev = reduce(VE, s.mx[0:S, 4 * g:4 * g + 4],
                                bk[g].ap[0:S, 0:4 * S].rearrange("p (q k) -> p q k", q=4), ALU.max, after=(last[g],))
                    bk[g].free = ev
                yield
                e_sh = split_max(s, S, ev, bk[3], s.shift1_x)
                yield
                for c in range(NC):
                    for j in range(2):
                        for g in range(ROWS):
                            r = slice(32 * g, 32 * g + 32)
                            at = (2 * c + j) * S
                            mm(bk[g].ap[0:S, at:at + S], s.kT[r, j, c, t], s.qT[r, c, t],
                               start=(c, j) == (0, 0), stop=False, after=(bk[g].free,), shared=True)
                for g in range(ROWS):
                    for q in range(4):
                        last[g] = mm(bk[g].ap[0:S, q * S:(q + 1) * S], shift1_w[:, 4 * g + q, :], s.shift1_x[:, :],
                                     start=False, stop=True, after=(e_sh,), shared=True, signal=q == 3)
                for g in range(ROWS):
                    e_E = act(s.E[0:S, 4 * g:4 * g + 4, :].rearrange("p q m -> p (q m)"), bk[g].ap[0:S, 0:4 * S],
                              ACT.Exp, after=(last[g],), scale=float(DH) ** -0.5)
                    bk[g].free = e_E
                yield
                for h in sorted(range(H), key=lambda h: place(h)[3]):
                    last = mm(bk[0].ap[0:S, h * (DH + 1):(h + 1) * (DH + 1)], s.E[0:S, place(h)[3], :], s.v[:, b, h, :],
                              after=(e_E, e_v), signal=h == H - 1)
                heads = bk[0].ap[0:S, 0:H * (DH + 1)].rearrange("p (h d) -> p h d", h=H)
                ev = recip(s.rden[0:S, :], heads[:, :, DH], after=(last,))
                ev = tt(VE, s.o[0:S, b, :].rearrange("p (h d) -> p h d", h=H), heads[:, :, 0:DH],
                        s.rden[0:S, :].unsqueeze(2).to_broadcast([S, H, DH]), ALU.mult, after=(ev,))
                bk[0].free = ev
                yield
            e_oT = transpose_tokens(s.o[0:S, :, :], s.aT, bk[1], ev)
            yield
            last = project_tokens(s.aT, W["a_o"], bk[2], after=(e_oT,))
            ev = tt(VE, s.r[:, :, :].rearrange("p b d -> p (b d)"), bk[2].ap[0:S, 0:NB * D],
                    s.xb[:, :, :].rearrange("p b d -> p (b d)"), ALU.add, after=(last, e_xb))
            bk[2].free = ev
            yield
            s.x_ready = layernorm(s, s.x, [ev, ev])

        def sub_quant(s, bk):
            e_xb = add_row(s, rows["n_bias"], s.x_ready)
            for b in range(NB):
                e_ms = act(s.prod[:, b, :], s.x[:, b, :], ACT.Square, after=(s.x_ready,),
                           accum_out=s.ms[:, b:b + 1])
            e_am = act(s.r[:, :, :], s.x[:, :, :], ACT.Abs, after=(s.x_ready,))
            e_am = reduce(VE, s.am[:, :], s.r[:, :, :], ALU.max, after=(e_am,))
            ev = ts(PO, s.ms[:, :], s.ms[:, :], 1.0 / D, ALU.mult, RMS_EPS, ALU.add, after=(e_ms,))
            ev = tt(PO, s.rms[:, :], s.ms[:, :], minus_half[0:S, 0:NB], ALU.pow, after=(ev,))
            ev = tt(VE, s.am2[:, :], s.am[:, :], s.rms[:, :], ALU.mult, after=(ev, e_am))
            ev = ts(VE, s.am2[:, :], s.am2[:, :], ACT_EPS, ALU.max, after=(ev,))
            e_os = ts(VE, s.os[:, :], s.am2[:, :], qscale[0:S, :], ALU.mult, after=(ev,))
            ev = recip(s.ra[:, :], s.am2[:, :], after=(ev,))
            ev = ts(VE, s.sc[:, :], s.ra[:, :], 127.0, ALU.mult, after=(ev,))
            for b in range(NB):
                e1 = ts(VE, s.y[:, b, :], s.x[:, b, :], s.rms[:, b:b + 1], ALU.mult, s.sc[:, b:b + 1], ALU.mult,
                        after=(ev,))
            e1 = ts(VE, s.y[:, :, :], s.y[:, :, :], ROUND, ALU.add, ROUND + 127.0, ALU.min, after=(e1,))
            e1 = ts(VE, s.yq[:, :, :], s.y[:, :, :], ROUND - 128.0, ALU.max, ROUND, ALU.subtract, after=(e1,))
            yield
            for c in range(NC):
                for b in range(NB):
                    at = (c * NB + b) * S
                    last = tr(bk[0].bf[:, at:at + S], s.yq[:, b, c * P:(c + 1) * P], ident_b[0:S, 0:S],
                              after=(e1, bk[0].free), signal=(c, b) == (NC - 1, NB - 1))
            bk[0].free = ev = act(s.yT[:, :, :].rearrange("p c t -> p (c t)"), bk[0].bf[:, 0:NC * T], after=(last,))
            yield
            last = project_tokens(s.yT, w8, bk[1], after=(ev,))
            ready = [stt(s.r[:, b, :], bk[1].ap[0:S, b * D:(b + 1) * D], s.os[:, b:b + 1], s.xb[:, b, :],
                         ALU.mult, ALU.add, after=(last, e_os, e_xb)) for b in range(NB)]
            bk[1].free = ready[-1]
            yield
            VE.now(lambda e, i: e.wait_ge(s_store[s.n], 16 * (i + 1)))
            s.x_ready = layernorm(s, s.out, ready)

        def store(s, tile):
            SY.wait(s.x_ready)
            SY.now(lambda e, i: e.dma_start(out[bass.ds(i * 2 + s.n, 1), :, :, :].rearrange("o p b d -> (o p) b d"),
                                            tile[:, :, :]).then_inc(s_store[s.n], 16))

        def load_group(e, turn):
            e.dma_start(xin[:, :, :], ins["x"][turn, :, :, :].rearrange("p b d -> p b d")
                        if isinstance(turn, int) else
                        ins["x"][bass.ds(turn, 1), :, :, :].rearrange("o p b d -> (o p) b d")).then_inc(s_xin, 16)

        def pick(name, n, turn):
            if isinstance(turn, int):
                return ins[name][turn * 2 + n, :, :, :]
            return ins[name][bass.ds(turn * 2 + n, 1), :, :, :].rearrange("o p b d -> (o p) b d")

        def load_masks(e, s, turn):
            e.dma_start(s.cell[:, :, :], pick("cell", s.n, turn)).then_inc(s_mask[s.n], 16)
            src = ins["seq"][turn * 2 + s.n:turn * 2 + s.n + 1, :] if isinstance(turn, int) else \
                ins["seq"][bass.ds(turn * 2 + s.n, 1), :]
            e.dma_start(s.seq[:, :, :].rearrange("p b k -> p (b k)"),
                        src.to_broadcast([S, NB * S2])).then_inc(s_mask[s.n], 16)

        def load_ctx(e, s, turn):
            e.dma_start(s.ctxT[:, :, :, :].rearrange("p b c k -> p b (c k)"),
                        pick("ctxT", s.n, turn)).then_inc(s_ctx[s.n], 16)
            e.dma_start(s.ctx[:, :, :, :].rearrange("p b j d -> p b (j d)"),
                        pick("ctx", s.n, turn)).then_inc(s_ctx[s.n], 16)

        def stream(s):
            bk = banks[4 * s.n:4 * s.n + 4]
            yield from sub_agent(s, bk)
            yield
            PO.now(lambda e, i: e.wait_ge(s_mask[s.n], 32 * (i + 1)))
            log_masks(s)
            SY.wait(s.mask_ready)
            SY.now(lambda e, i: load_masks(e, s, i + 1))
            PE.now(lambda e, i: e.wait_ge(s_ctx[s.n], 32 * (i + 1)))
            if LAST_LAYER >= 2:
                yield from cross(s, bk, W["x_k"], None, rows["x_bk"], None, W["x_o"], rows["x_bo"], True)
                yield
            if LAST_LAYER >= 3:
                yield from sub_select(s, bk)
                yield
            if LAST_LAYER >= 4:
                yield from sub_local(s, bk)
                yield
            if LAST_LAYER >= 5:
                yield from cross(s, bk, wqk, bqk, wqbk, bqbk, wvo, bvo, False)
                yield
            SY.wait(s.ctx_used if LAST_LAYER >= 2 else s.x_ready)
            SY.now(lambda e, i: load_ctx(e, s, i + 1))
            if LAST_LAYER >= 6:
                yield from sub_quant(s, bk)
                store(s, s.out)
            else:
                VE.now(lambda e, i: e.wait_ge(s_store[s.n], 16 * (i + 1)))
                s.x_ready = copy(VE, s.out[:, :, :], s.x[:, :, :], after=(s.x_ready,))
                store(s, s.out)
            yield

        def agent_next():
            while not all(s.took for s in streams):
                yield
            kept = [ev for s in streams for ev in s.agent_used]
            SY.wait(*kept)
            SY.now(lambda e, i: load_group(e, i + 1))
            for _ in range(AGENT_START):
                yield
            yield from agent(lambda e, i: e.wait_ge(s_xin, 16 * (i + 2)), kept)

        AGENT_START = 6 if LAST_LAYER >= 3 else 0

        n_const = 0

        def load(dst, src):
            nonlocal n_const
            n_const += 16
            SY.now(lambda e, i: e.dma_start(dst, src).then_inc(s_const, 16))

        SY.now(lambda e, i: load_group(e, 0))
        for n in WEIGHTS:
            load(W[n][:, :, :], ins[n].rearrange("(c p) n -> p c n", p=P))
        for n in ROWVECS:
            load(rows[n][:, :], ins[n].to_broadcast([P, D]))
        for n in COLVECS:
            load(cols[n][:, :], ins[n])
        load(w8_i.rearrange("p (c n) -> p c n", c=NC), ins["w8"].rearrange("(c p) n -> p c n", p=P))
        load(wscale[:, :], ins["wscale"].to_broadcast([P, 1]))
        for n, t in (("ident", ident), ("ident_b", ident_b), ("before", before), ("slots", slots), ("parity", parity),
                     ("edge_key", edge_key), ("edge_mask", edge_mask)):
            load(t[:, :], ins[n])
        for n, t in (("pick_batch", pick_batch), ("shift1_w", shift1_w), ("shift0_w", shift0_w)):
            load(t[:, :, :], ins[n])
        for s in streams:
            load(s.shift1_x[:, :], ins["shift1_x"])
        for s in streams:
            SY.now(lambda e, i, s=s: load_masks(e, s, 0))
            SY.now(lambda e, i, s=s: load_ctx(e, s, 0))
            SY.now(lambda e, i, s=s: e.sem_inc(s_store[s.n], 16))

        VE.put(lambda e: e.memset(ones[:, :], 1.0))
        VE.put(lambda e: e.memset(minus_half[:, :], -0.5))
        for s in streams:
            VE.put(lambda e, s=s: e.memset(s.p[:, :, :], 0.0))
            VE.put(lambda e, s=s: e.memset(s.v[:, :, :, :], 1.0))
            VE.put(lambda e, s=s: e.memset(s.v0[:, :, :], 1.0))
            VE.put(lambda e, s=s: e.memset(s.shift0_x[:, :], 1.0))
        for q in (VE, PE, AC, PO):
            q.now(lambda e, i: e.wait_ge(s_const, n_const))

        def spread(bank, vec, w, at=0, cols_=D):
            for c in range(NC):
                last = mm(bank.ap[:, at:at + cols_], vec[:, c:c + 1].to_broadcast([P, P]), w[:, c, 0:cols_],
                          start=c == 0, stop=c == NC - 1, after=(bank.free,), signal=c == NC - 1)
            return last

        inv = float(D) ** -0.5
        last = spread(banks[0], cols["w_conv1"], W["w_q0"])
        banks[0].free = e_aw = copy(VE, agent_w[:, :], banks[0].ap[:, 0:D], after=(last,))
        last = spread(banks[1], cols["a_bv"], W["a_o"])
        banks[1].free = tt(VE, bo1[:, :], banks[1].ap[:, 0:D], rows["a_bo"][:, :], ALU.add, after=(last,))
        last = spread(banks[2], cols["c_bk"], W["c_qT"])
        banks[2].free = ts(VE, wqbk[:, :], banks[2].ap[:, 0:D], inv, ALU.mult, after=(last,))
        last = spread(banks[4], cols["c_bv"], W["c_o"])
        banks[4].free = tt(VE, bvo[:, :], banks[4].ap[:, 0:D], rows["c_bo"][:, :], ALU.add, after=(last,))
        for c in range(NC):
            last = mm(banks[5].ap[:, 0:1], cols["c_bk"][:, c:c + 1].to_broadcast([P, P]), cols["c_bq"][:, c:c + 1],
                      start=c == 0, stop=c == NC - 1, after=(banks[5].free,), signal=c == NC - 1)
        banks[5].free = ts(VE, bqbk[:, :], banks[5].ap[:, 0:1], inv, ALU.mult, after=(last,))
        for e in range(NC):
            for c in range(NC):
                last = mm(banks[6].ap[:, e:e + 1], W["c_kT"][:, c, e * P:(e + 1) * P], cols["c_bq"][:, c:c + 1],
                          start=c == 0, stop=c == NC - 1, signal=(e, c) == (NC - 1, NC - 1))
        banks[6].free = ts(VE, bqk[:, :], banks[6].ap[:, 0:NC], inv, ALU.mult, after=(last,))
        for dst, a, b_, scale in ((wqk, W["c_qT"], W["c_kT"], inv), (wvo, W["c_vT"], W["c_o"], 1.0)):
            for e in range(NC):
                for c in range(NC):
                    last = mm(banks[7].ap[:, e * D:(e + 1) * D], a[:, c, e * P:(e + 1) * P], b_[:, c, :],
                              start=c == 0, stop=c == NC - 1, after=(banks[7].free,), signal=(e, c) == (NC - 1, NC - 1))
            banks[7].free = ts(VE, dst[:, :, :].rearrange("p c n -> p (c n)"), banks[7].ap[:, 0:NC * D], scale,
                               ALU.mult, after=(last,))
        for j in range(2):
            ts(VE, bkp[:, j, :], cols["a_bk"][:, :], parity[:, j:j + 1], ALU.mult)
        copy(VE, w8[:, :, :].rearrange("p c n -> p (c n)"), w8_i)
        ts(VE, qscale[:, :], wscale[:, :], 1.0 / 127.0, ALU.mult)
        VE.wait(e_aw)
        for _ in agent(lambda e, i: e.wait_ge(s_xin, 16), ()):
            pass

        prologue = {q.name: list(q.steps) for q in (*engines, SY)}
        prologue_counts = {q.name: q.count for q in engines}
        for q in (*engines, SY):
            q.restart()
        for k in banks:
            k.free = None

        for s in streams:
            s.took = False
            s.prod_used = None
            s.agent_used = ()
        running = [stream(s) for s in streams]
        extra = agent_next()
        alive = list(running)
        while alive or extra is not None:
            for g in list(alive):
                try:
                    next(g)
                except StopIteration:
                    alive.remove(g)
            for s in streams:
                s.took = bool(s.agent_used)
            if extra is not None:
                try:
                    next(extra)
                except StopIteration:
                    extra = None
        body_counts = {q.name: q.count for q in engines}

        def meet(e, q, counts):
            if q in engines:
                e.wait_ge(q.sem, counts[q.name])
            if q is PO:
                e.wait_ge(s_arrive, len(s_go))
                for other in engines:
                    e.sem_clear(other.sem)
                e.sem_clear(s_arrive)
                for n in s_go:
                    e.sem_inc(s_go[n], 1)
            else:
                e.sem_inc(s_arrive, 1)
                e.wait_ge(s_go[q.name], 1)
                e.sem_clear(s_go[q.name])

        def emit(e, q):
            for step in prologue[q.name]:
                step(e, 0)
            meet(e, q, prologue_counts)
            with e.Fori(0, NI) as i:
                q.run(e, i)
                meet(e, q, body_counts)
            if q is SY:
                for s in streams:
                    e.wait_ge(s_store[s.n], 16 * (NI + 1))
                    e.wait_ge(s_mask[s.n], 32 * (NI + 1))
                    e.wait_ge(s_ctx[s.n], 32 * (NI + 1))
                e.wait_ge(s_xin, 16 * (NI + 1))

        block = ctx.enter_context(nc.Block())

        @block.sync
        def _(e):
            emit(e, SY)

        @block.gpsimd
        def _(e):
            emit(e, PO)

        @block.scalar
        def _(e):
            emit(e, AC)

        @block.tensor
        def _(e):
            emit(e, PE)

        @block.vector
        def _(e):
            emit(e, VE)


WEIGHTS = ["w_q0", "w_k0", "w_v0", "w_v0T", "x_k", "x_o", "f_q", "f_k", "f_v", "f_o", "a_q", "a_k", "a_v", "a_o",
           "c_qT", "c_kT", "c_vT", "c_o"]
ROWVECS = ["x_bk", "x_bo", "f_wg", "a_bo", "c_bo", "n_bias"]
COLVECS = ["w_conv1", "a_bq", "a_bk", "a_bv", "c_bq", "c_bk", "c_bv"]


def constants():
    bf = mybir.dt.np(BF16)
    t = np.arange(S)
    edge = np.concatenate([np.arange(NEDGE), np.arange(S - NEDGE, S)])
    one_key = (edge[:, None] == t[None, :]).astype(np.float32)
    mask = np.where(np.abs(edge[:, None] - t[None, :]) > BAND, NEG, 0.0).astype(np.float32)
    shift1_w = np.zeros((2 * H + NM, H, S), np.float32)
    shift0_w = np.zeros((2 * H + 1, H, SLOT), np.float32)
    for h in range(H):
        for part in range(2):
            shift1_w[part * H + h, h] = 1.0
            shift0_w[part * H + h, h] = 1.0
    shift1_w[2 * H:] = one_key[:, None, :]
    shift0_w[2 * H, :, CAP:] = NEG
    slots = np.where(np.arange(SLOT) < CAP, np.arange(SLOT), 1000 + np.arange(SLOT)).astype(np.float32)
    pick = np.zeros((G, G, S), np.float32)
    for b in range(G):
        pick[b, b] = 1.0
    row = np.arange(P) // DH % 2
    return {
        "ident": np.eye(P, dtype=np.float32), "ident_b": np.eye(P).astype(bf),
        "before": (t[None, :] < t[:, None]).astype(np.float32), "slots": np.tile(slots, (S, 1)),
        "parity": np.stack([row == 0, row == 1], 1).astype(np.float32),
        "pick_batch": pick, "edge_key": one_key.astype(bf), "edge_mask": mask.astype(bf),
        "shift1_w": shift1_w.astype(bf), "shift0_w": shift0_w.astype(bf),
        "shift1_x": np.concatenate([np.zeros((2 * H, S), np.float32), mask]).astype(bf),
    }


def kernel(x, ctx_1024, mask_BxSxS2_ff1, mask_BxS2_ff1, L0_attn_w_qkv, L0_attn_w_conv1, L0_xattn_W_k, L0_xattn_b_k,
           L0_xattn_W_o, L0_xattn_b_o, L0_ffn_Wg, L0_ffn_Wq, L0_ffn_Wk, L0_ffn_Wv, L0_ffn_Wo, L1_attn_Wq, L1_attn_bq,
           L1_attn_Wk, L1_attn_bk, L1_attn_Wv, L1_attn_bv, L1_attn_Wo, L1_attn_bo, L1_xattn_Wq, L1_xattn_bq,
           L1_xattn_Wk, L1_xattn_bk, L1_xattn_Wv, L1_xattn_bv, L1_xattn_Wo, L1_xattn_bo, L1_ffn_w_int8,
           L1_ffn_weight_scale, L1_ffn_bias):
    import concourse.bacc as _bacc
    from concourse.bass_utils import run_bass_kernel_spmd as _run

    def arr(a):
        return np.ascontiguousarray(np.asarray(a))

    def more(a):
        return np.concatenate([a, a[:G]], 0)

    x, c = arr(x), arr(ctx_1024)
    cpad = np.zeros((B, S2C * P, D), c.dtype)
    cpad[:, :S2] = c
    w = arr(L0_attn_w_qkv)

    def streams_first(a):
        a = more(a).reshape(-1, NB, *a.shape[1:])
        return arr(np.moveaxis(a, 1, 2))

    def col(v):
        return arr(arr(v).reshape(NC, P).T)

    def row(v):
        return arr(v).reshape(1, D)

    arrays = {
        "x": arr(np.moveaxis(more(x).reshape(-1, G, S, D), 1, 2)),
        "ctx": streams_first(cpad.reshape(B, S2C, P, D).transpose(0, 2, 1, 3).reshape(B, P, S2C * D)),
        "ctxT": streams_first(c.transpose(0, 2, 1).reshape(B, NC, P, S2).transpose(0, 2, 1, 3).reshape(B, P, NC * S2)),
        "cell": streams_first(arr(mask_BxSxS2_ff1)),
        "seq": arr(more(arr(mask_BxS2_ff1)).reshape(-1, NB * S2)),
        "w_q0": w[:D], "w_k0": w[D:2 * D].T, "w_v0": w[2 * D:], "w_v0T": w[2 * D:].T,
        "x_k": L0_xattn_W_k, "x_o": arr(L0_xattn_W_o).T,
        "f_q": L0_ffn_Wq, "f_k": L0_ffn_Wk, "f_v": L0_ffn_Wv, "f_o": L0_ffn_Wo,
        "a_q": arr(L1_attn_Wq).T, "a_k": arr(L1_attn_Wk).T, "a_v": arr(L1_attn_Wv).T, "a_o": arr(L1_attn_Wo).T,
        "c_qT": arr(L1_xattn_Wq).T, "c_kT": arr(L1_xattn_Wk).T, "c_vT": arr(L1_xattn_Wv).T, "c_o": L1_xattn_Wo,
        "x_bk": row(L0_xattn_b_k), "x_bo": row(L0_xattn_b_o), "f_wg": row(L0_ffn_Wg), "a_bo": row(L1_attn_bo),
        "c_bo": row(L1_xattn_bo), "n_bias": row(L1_ffn_bias),
        "w_conv1": col(L0_attn_w_conv1), "a_bq": col(L1_attn_bq), "a_bk": col(L1_attn_bk), "a_bv": col(L1_attn_bv),
        "c_bq": col(L1_xattn_bq), "c_bk": col(L1_xattn_bk), "c_bv": col(L1_xattn_bv),
        "w8": arr(L1_ffn_w_int8).T, "wscale": arr(L1_ffn_weight_scale).reshape(1, 1),
        **constants(),
    }
    nc = _bacc.Bacc("TRN2", target_bir_lowering=False, num_devices=1)
    ins, data = {}, {}
    for name, a in arrays.items():
        a = arr(a)
        data["in_" + name] = a
        ins[name] = nc.dram_tensor("in_" + name, a.shape, mybir.dt.from_np(a.dtype), kind="ExternalInput").ap()
    out = nc.dram_tensor("out", (B // NB, S, NB, D), F32, kind="ExternalOutput").ap()
    program(nc, ins, out)
    r = _run(nc, [data], core_ids=[0])
    got = arr(r.results[0]["out"])
    return arr(np.moveaxis(got, 2, 1)).reshape(B, S, D)
```

```python
import numpy as np
from contextlib import ExitStack

import concourse.bass as bass
from concourse import mybir

F32 = mybir.dt.float32
BF16 = mybir.dt.bfloat16
I32 = mybir.dt.int32
ALU = mybir.AluOpType
ACT = mybir.ActivationFunctionType
AX = mybir.AxisListType.X

B, S, D, S2 = 32, 100, 256, 361
H, DH = 16, 16
P = 128
NC = D // P
G = 4
NI = B // G
NB = 2
T = NB * S
S2C = 3
CAP = S // 2
assert NB * CAP == S
BAND = 64
NEDGE = S - 1 - BAND
NM = 2 * NEDGE
ROWS = P // 32
NEG = -1.0e30
TINY = 2.0 ** -63
ROUND = 1.5 * 2.0 ** 23
LN_EPS, RMS_EPS, ACT_EPS = 1e-5, 1e-6, 1e-5


class Queue:

    def __init__(self, name, sem):
        self.name, self.sem = name, sem
        self.restart()

    def restart(self):
        self.steps, self.count, self.seen = [], 0, {}

    def wait(self, *events):
        for sem, value in events:
            if self.seen.get(id(sem), 0) < value:
                self.seen[id(sem)] = value
                self.steps.append(lambda e, i, sem=sem, value=value: e.wait_ge(sem, value))

    def put(self, make, after=(), signal=True):
        self.wait(*[ev for ev in after if ev is not None])
        if not signal:
            self.steps.append(lambda e, i: make(e))
            return None
        self.count += 1
        self.steps.append(lambda e, i: make(e).then_inc(self.sem, 1))
        return (self.sem, self.count)

    def now(self, make):
        self.steps.append(make)

    def run(self, e, i=None):
        for step in self.steps:
            step(e, i)


class Bank:

    def __init__(self, ap):
        self.ap, self.bf, self.free, self.held = ap, ap.bitcast(BF16), None, False


def program(nc, ins, out):
    ctx = ExitStack()
    with ctx:
        def sb(name, shape, dt=F32):
            return ctx.enter_context(nc.sbuf_tensor(name, list(shape), dt))

        def sem(name):
            return ctx.enter_context(nc.semaphore(name))

        W = {n: sb(n, [P, NC, D]) for n in WEIGHTS if n not in EARLY}
        rows = {n: sb(n + "_r", [P, D]) for n in ROWVECS}
        cols = {n: sb(n + "_c", [P, NC]) for n in COLVECS}
        w8 = sb("w8", [P, NC, D], BF16)
        wscale = sb("wscale", [P, 1])
        qscale = sb("qscale", [P, 1])
        ident = sb("ident", [P, P])
        ident_b = sb("ident_b", [P, P], BF16)
        ones = sb("ones", [P, P])
        before = sb("before", [S, S])
        slots = sb("slots", [S, NB, S])
        parity = sb("parity", [P, 2])
        pick_batch = sb("pick_batch", [G, G, S])
        band_w = sb("band_w", [NM, S], BF16)
        band_x = sb("band_x", [NM, S], BF16)
        pair_w = sb("pair_w", [P, S], BF16)
        pair_x = sb("pair_x", [P, S], BF16)
        pick_head = sb("pick_head", [2 * H, H, S], BF16)
        agent_w = sb("agent_w", [P, D])
        bo1 = sb("bo1", [P, D])
        wqk = sb("wqk", [P, NC, D])
        bqk = sb("bqk", [P, NC])
        wqbk = sb("wqbk", [P, D])
        bqbk = sb("bqbk", [P, 1])
        wvo = sb("wvo", [P, NC, D])
        bvo = sb("bvo", [P, D])
        bkp = sb("bkp", [P, 2, NC])

        xin = sb("xin", [S, G, D])
        ag = sb("ag", [S, G])
        tok = sb("tok", [S, G])
        tokd = sb("tokd", [S, G])
        toke = sb("toke", [S, G])
        tokr = sb("tokr", [S, G])
        ajunk = sb("ajunk", [S, D])
        agd = sb("agd", [S, G, G])
        yrow = sb("yrow", [G, D])
        yT = sb("yT", [P, NC, G])
        arow = sb("arow", [G, D])
        arow2 = sb("arow2", [G, D])
        astat = sb("astat", [G, 8])
        aT = sb("aT", [P, NC, G])
        zrow = sb("zrow", [G, D])
        zT = sb("zT", [P, NC, G, G])
        only = sb("only", [P, G, G])
        xinT = sb("xinT", [P, NC, G * S])
        lrow = sb("lrow", [G, S])
        lrow2 = sb("lrow2", [G, S])
        acol = sb("acol", [S, G, G])
        avT = sb("avT", [P, NC, G])
        agent_v = sb("agent_v", [G, D])

        class Stream:

            def __init__(s, n):
                s.n = n
                s.x = sb(f"x{n}", [S, NB, D])
                s.xb = sb(f"xb{n}", [S, NB, D])
                s.r = sb(f"r{n}", [S, NB, D])
                s.xT = sb(f"xT{n}", [P, NC, T])
                s.aT = sb(f"aT{n}", [P, NC, T])
                s.qT = sb(f"qT{n}", [P, NC, T])
                s.kT = sb(f"kT{n}", [P, 2, NC, T])
                s.v = sb(f"v{n}", [S, NB, H, 2 * DH])
                s.e = sb(f"e{n}", [P, H, S])
                s.eT = sb(f"eT{n}", [S, H, S])
                s.ctx = sb(f"ctx{n}", [P, NB, S2C, D])
                s.ctxT = sb(f"ctxT{n}", [P, NB, NC, S2])
                s.cell = sb(f"cell{n}", [S, NB, S2])
                s.seq = sb(f"seq{n}", [S, NB, S2])
                s.lmask = sb(f"lmask{n}", [S, NB, S2])
                s.sm = sb(f"sm{n}", [S, NB, S2])
                s.p = sb(f"p{n}", [S, NB, S2C * P])
                s.pT = sb(f"pT{n}", [P, S2C, S])
                s.prod = sb(f"prod{n}", [S, NB, D])
                s.qb = sb(f"qb{n}", [S, NB])
                s.bn = sb(f"bn{n}", [S, NB, 6])
                s.mv = sb(f"mv{n}", [S, NB, 2])
                s.ve = sb(f"ve{n}", [S, NB])
                s.rstd = sb(f"rstd{n}", [S, NB])
                s.mx = sb(f"mx{n}", [S, H])
                s.mx2 = sb(f"mx2{n}", [P, NB])
                s.nb = sb(f"nb{n}", [S, NB])
                s.sum = sb(f"sum{n}", [S, NB])
                s.rsum = sb(f"rsum{n}", [S, NB])
                s.hl = sb(f"hl{n}", [S, 2 * H], BF16)
                s.den = sb(f"den{n}", [S, H])
                s.rden = sb(f"rden{n}", [S, H])
                s.z = sb(f"z{n}", [S, NB])
                s.ez = sb(f"ez{n}", [S, NB])
                s.gp = sb(f"gp{n}", [S, NB])
                s.gate = sb(f"gate{n}", [S, NB])
                s.dg = sb(f"dg{n}", [S, NB, S])
                s.tie = sb(f"tie{n}", [S, S])
                s.above = sb(f"above{n}", [S, S])
                s.rank = sb(f"rank{n}", [S, NB])
                s.sel = sb(f"sel{n}", [S, NB, S])
                s.selT = sb(f"selT{n}", [S, NB, S])
                s.w0 = sb(f"w0{n}", [S, D])
                s.shift = sb(f"shift{n}", [2 * H, S], BF16)
                s.ms = sb(f"ms{n}", [S, NB])
                s.rms = sb(f"rms{n}", [S, NB])
                s.am = sb(f"am{n}", [S, NB])
                s.am2 = sb(f"am2{n}", [S, NB])
                s.sc = sb(f"sc{n}", [S, NB])
                s.ra = sb(f"ra{n}", [S, NB])
                s.os = sb(f"os{n}", [S, NB])
                s.yq = sb(f"yq{n}", [S, NB, D], BF16)
                s.yT = sb(f"yT{n}", [P, NC, T], BF16)
                s.out = sb(f"out{n}", [S, NB, D])

        streams = []
        for n in range(G // NB):
            s = Stream(n)
            s.y = s.prod
            s.x_ready, s.masks_in_use, s.mask_used = None, False, ()
            streams.append(s)

        for k, n in enumerate(EARLY):
            room = streams[k // 3].e[:, :, :].rearrange("p h s -> p (h s)")
            W[n] = room[:, k % 3 * NC * D:(k % 3 + 1) * NC * D].rearrange("p (c n) -> p c n", c=NC)
        w8_i = W.pop("w8_i").bitcast(I32)
        psum = ctx.enter_context(nc.psum_tensor("psum", [P, 8, 512], F32))
        banks = [Bank(psum[:, k, :]) for k in range(8)]

        PE, VE, AC, PO = (Queue(n, sem("s_" + n)) for n in ("tensor", "vector", "scalar", "gpsimd"))
        SY = Queue("sync", None)
        engines = [PE, VE, AC, PO]
        s_const = sem("s_const")
        s_xin = sem("s_xin")
        s_ctx = [sem(f"s_ctx{n}") for n in range(G // NB)]
        s_mask = [sem(f"s_mask{n}") for n in range(G // NB)]
        s_store = [sem(f"s_store{n}") for n in range(G // NB)]
        s_arrive = sem("s_arrive")
        s_go = {n: sem("s_go_" + n) for n in ("tensor", "vector", "scalar", "sync")}

        def mm(dst, w, x, start=True, stop=True, after=(), signal=False, shared=False):
            return PE.put(lambda e: e.matmul(dst, w, x, start=start, stop=stop, skip_group_check=shared),
                          after, signal)

        def tr(dst, src, idn, after=(), signal=False):
            return PE.put(lambda e: e.transpose(dst, src, idn), after, signal)

        def act(dst, src, fn=ACT.Copy, after=(), **kw):
            return AC.put(lambda e: e.activation(dst, src, fn, **kw), after)

        def copy(q, dst, src, after=()):
            if q is AC:
                return act(dst, src, after=after)
            return q.put(lambda e: e.tensor_copy(dst, src), after)

        def ts(q, dst, src, s1, op0, s2=None, op1=None, after=()):
            if op1 is None:
                return q.put(lambda e: e.tensor_scalar(dst, src, s1, None, op0), after)
            return q.put(lambda e: e.tensor_scalar(dst, src, s1, s2, op0, op1), after)

        def tt(q, dst, a, b, op, after=()):
            return q.put(lambda e: e.tensor_tensor(dst, a, b, op), after)

        def stt(dst, a, s1, b, op0, op1, after=(), **kw):
            return VE.put(lambda e: e.scalar_tensor_tensor(dst, a, s1, b, op0, op1, **kw), after)

        def reduce(q, dst, src, op, after=()):
            return q.put(lambda e: e.tensor_reduce(dst, src, AX, op), after)

        def recip(dst, src, after=()):
            return VE.put(lambda e: e.reciprocal(dst, src), after)

        def transpose_tokens(src, dst, bank, ready):
            for c in range(NC):
                for b in range(NB):
                    last = tr(bank.ap[:, (c * NB + b) * S:(c * NB + b + 1) * S],
                              src[:, b, c * P:(c + 1) * P], ident[0:S, 0:S],
                              after=(ready, bank.free), signal=(c, b) == (NC - 1, NB - 1))
            bank.free = act(dst[:, :, :].rearrange("p c t -> p (c t)"), bank.ap[:, 0:NC * T], after=(last,))
            return bank.free

        def project(w, xT, bank, n, at=0, after=()):
            for e in range(NC):
                for c in range(NC):
                    last = mm(bank.ap[:, at + e * n:at + (e + 1) * n], w[:, c, e * P:(e + 1) * P], xT[:, c, 0:n],
                              start=c == 0, stop=c == NC - 1, after=(*after, bank.free),
                              signal=(e, c) == (NC - 1, NC - 1))
            return last

        def project_tokens(xT, w, bank, after=()):
            for b in range(NB):
                for c in range(NC):
                    last = mm(bank.ap[0:S, b * D:(b + 1) * D], xT[:, c, b * S:(b + 1) * S], w[:, c, :],
                              start=c == 0, stop=c == NC - 1, after=(*after, bank.free),
                              signal=(b, c) == (NB - 1, NC - 1))
            return last

        def layernorm(s, dst, ready, after=()):
            st = [VE.put(lambda e, b=b: e.bn_stats(s.bn[:, b, :], s.r[:, b, :]), after=(ready[b],)) for b in range(NB)]
            for b in range(NB):
                ag_ = VE.put(lambda e, b=b: e.bn_aggr(s.mv[:, b, :], s.bn[:, b, :]), after=(st[b],))
            ev = ts(PO, s.ve[:, :], s.mv[:, :, 1], LN_EPS, ALU.add, after=(ag_,))
            ev = tt(PO, s.rstd[:, :], s.ve[:, :], minus_half[0:S, 0:NB], ALU.pow, after=(ev,))
            yield
            for b in range(NB):
                last = ts(VE, dst[:, b, :], s.r[:, b, :], s.mv[:, b, 0:1], ALU.subtract,
                          s.rstd[:, b:b + 1], ALU.mult, after=(ev, *after))
            return last

        def add_row(s, row, ready):
            return tt(PO, s.xb[:, :, :], s.x[:, :, :], row[0:S, :].unsqueeze(1).to_broadcast([S, NB, D]),
                      ALU.add, after=(ready,))

        def const_score(s, row, ready):
            ev = tt(PO, s.prod[:, :, :], s.x[:, :, :], row[0:S, :].unsqueeze(1).to_broadcast([S, NB, D]),
                    ALU.mult, after=(ready,))
            for b in range(NB):
                last = act(s.prod[:, b, :], s.prod[:, b, :], after=(ev,), accum_out=s.qb[:, b:b + 1])
            s.prod_used = last
            return last

        minus_half = sb("minus_half", [P, NB])

        def agent(loaded, kept):
            bank = banks[3]
            yield from when_free(bank)
            AC.now(loaded)
            VE.now(loaded)
            PE.now(loaded)
            for b in range(G):
                ev = stt(ajunk[:, :], xin[:, b, :], 1.0, agent_w[0:S, :], ALU.mult, ALU.mult,
                         after=(VE_last(),), accum_out=ag[:, b:b + 1])
            e1 = tt(VE, tokd[:, :], ag[:, :], ag[:, :], ALU.subtract, after=(ev,))
            e2 = act(toke[:, :], tokd[:, :], ACT.Exp, after=(e1,))
            yield from when_free(bank)
            e1 = tt(VE, agd[:, :, :], only[0:S, :, :], ag[:, :].unsqueeze(2).to_broadcast([S, G, G]), ALU.mult,
                    after=(ev,))
            for b in range(G):
                last = mm(bank.ap[0:G, 0:D], agd[:, b, :], xin[:, b, :], start=b == 0, stop=b == G - 1,
                          after=(e1, bank.free), signal=b == G - 1)
            bank.free = ev = ts(VE, yrow[:, :], bank.ap[0:G, 0:D], float(D) ** -0.5, ALU.mult, after=(last,))
            e1 = recip(tokr[:, :], toke[:, :], after=(e2,))
            s_tok[0] = tt(VE, tok[:, :], toke[:, :], tokr[:, :], ALU.mult, after=(e1, *kept))
            yield from when_free(bank)
            rows_to_columns(yrow, yT[:, :, :].rearrange("p c b -> p (c b)"), bank, ev)
            yield from when_free(bank)
            for c in range(NC):
                last = mm(bank.ap[0:G, 0:D], yT[:, c, :], W["w_k0"][:, c, :], start=c == 0, stop=c == NC - 1,
                          after=(bank.free,), signal=c == NC - 1)
            e1 = reduce(VE, astat[:, 0:1], bank.ap[0:G, 0:D], ALU.max, after=(last,))
            e1 = ts(VE, astat[:, 1:2], astat[:, 0:1], -1.0, ALU.mult, after=(e1,))
            bank.free = e1 = act(arow[:, :], bank.ap[0:G, 0:D], ACT.Exp, after=(e1,), bias=astat[:, 1:2],
                                 accum_out=astat[:, 2:3])
            yield from when_free(bank)
            e1 = recip(astat[:, 3:4], astat[:, 2:3], after=(e1,))
            e1 = ts(VE, arow2[:, :], arow[:, :], astat[:, 3:4], ALU.mult, after=(e1,))
            rows_to_columns(arow2, aT[:, :, :].rearrange("p c b -> p (c b)"), bank, e1)
            yield from when_free(bank)
            for c in range(NC):
                last = mm(bank.ap[0:G, 0:D], aT[:, c, :], W["w_v0"][:, c, :], start=c == 0, stop=c == NC - 1,
                          after=(bank.free,), signal=c == NC - 1)
            bank.free = ev = copy(VE, zrow[:, :], bank.ap[0:G, 0:D], after=(last,))
            yield from when_free(bank)
            for c in range(NC):
                last = tr(bank.ap[:, c * G:(c + 1) * G], zrow[:, c * P:(c + 1) * P], ident[0:G, 0:G],
                          after=(ev, bank.free), signal=c == NC - 1)
            for c in range(NC):
                bank.free = ez = tt(VE, zT[:, c, :, :], only[:, :, :],
                                    bank.ap[:, c * G:(c + 1) * G].unsqueeze(2).to_broadcast([P, G, G]), ALU.mult,
                                    after=(last,))
            yield from when_free(bank)
            for c in range(NC):
                for b in range(G):
                    last = tr(bank.ap[:, b * S:(b + 1) * S], xin[:, b, c * P:(c + 1) * P], ident[0:S, 0:S],
                              after=(bank.free,), signal=b == G - 1)
                bank.free = ev = act(xinT[:, c, :], bank.ap[:, 0:G * S], after=(last,))
                yield from when_free(bank)
            for b in range(G):
                for c in range(NC):
                    last = mm(bank.ap[0:G, 0:S], zT[:, c, b, :], xinT[:, c, b * S:(b + 1) * S],
                              start=(b, c) == (0, 0), stop=(b, c) == (G - 1, NC - 1), after=(ez, ev, bank.free),
                              signal=(b, c) == (G - 1, NC - 1))
            e1 = reduce(VE, astat[:, 4:5], bank.ap[0:G, 0:S], ALU.max, after=(last,))
            e1 = ts(VE, astat[:, 5:6], astat[:, 4:5], -1.0, ALU.mult, after=(e1,))
            bank.free = e1 = act(lrow[:, :], bank.ap[0:G, 0:S], ACT.Exp, after=(e1,), bias=astat[:, 5:6],
                                 accum_out=astat[:, 6:7])
            yield from when_free(bank)
            e1 = recip(astat[:, 7:8], astat[:, 6:7], after=(e1,))
            e1 = ts(VE, lrow2[:, :], lrow[:, :], astat[:, 7:8], ALU.mult, after=(e1,))
            last = tr(bank.ap[0:S, 0:G], lrow2[:, :], ident[0:G, 0:G], after=(e1, bank.free), signal=True)
            bank.free = e1 = tt(VE, acol[:, :, :], only[0:S, :, :],
                                bank.ap[0:S, 0:G].unsqueeze(2).to_broadcast([S, G, G]), ALU.mult, after=(last,))
            yield from when_free(bank)
            for b in range(G):
                last = mm(bank.ap[0:G, 0:D], acol[:, b, :], xin[:, b, :], start=b == 0, stop=b == G - 1,
                          after=(e1, bank.free), signal=b == G - 1)
            bank.free = ev = copy(VE, yrow[:, :], bank.ap[0:G, 0:D], after=(last,))
            yield from when_free(bank)
            rows_to_columns(yrow, yT[:, :, :].rearrange("p c b -> p (c b)"), bank, ev)
            yield from when_free(bank)
            for c in range(NC):
                last = mm(bank.ap[0:G, 0:D], yT[:, c, :], W["w_v0T"][:, c, :], start=c == 0, stop=c == NC - 1,
                          after=(bank.free,), signal=c == NC - 1)
            bank.free = s_tok[1] = copy(VE, agent_v[:, :], bank.ap[0:G, 0:D], after=(last, *kept))
            yield

        s_tok = [None, None, 1]

        def when_free(bank):
            yield
            while bank.held:
                yield

        def rows_to_columns(src, dst, bank, ready):
            for c in range(NC):
                last = tr(bank.ap[:, c * G:(c + 1) * G], src[:, c * P:(c + 1) * P], ident[0:G, 0:G],
                          after=(ready, bank.free), signal=c == NC - 1)
            bank.free = copy(VE, dst, bank.ap[:, 0:NC * G], after=(last,))

        def VE_last():
            return (VE.sem, VE.count) if VE.count else None

        def sub_agent(s, bk):
            ready = [None] * NB
            for b in range(NB):
                last = mm(bk[0].ap[0:S, b * D:(b + 1) * D], pick_batch[:, NB * s.n + b, :], agent_v[:, :],
                          after=(s_tok[1], bk[0].free), signal=b == NB - 1)
            for b in range(NB):
                n = NB * s.n + b
                ready[b] = stt(s.r[:, b, :], bk[0].ap[0:S, b * D:(b + 1) * D], tok[:, n:n + 1], xin[:, n, :],
                               ALU.mult, ALU.add, after=(last, s_tok[0], s.x_ready))
            bk[0].free = ready[-1]
            s.agent_used = (last, ready[-1])
            yield
            s.x_ready = yield from layernorm(s, s.x, ready)

        def log_masks(turn):
            yield
            for s in streams:
                while s.masks_in_use:
                    yield
                PO.now(lambda e, i, s=s: e.wait_ge(s_mask[s.n], 32 * (i + turn)))
                s.e_mask = tt(PO, s.cell[:, :, :], s.cell[:, :, :], s.seq[:, :, :], ALU.mult)
            yield
            for s in streams:
                ev = s.e_mask
                s.e_zero = ts(VE, s.lmask[:, :, :], s.cell[:, :, :], 0.0, ALU.is_equal, 3.0 * NEG, ALU.mult,
                              after=(ev, *s.mask_used))
                s.e_mask = ts(VE, s.sm[:, :, :], s.cell[:, :, :], TINY, ALU.max, after=(ev, *s.mask_used))
            SY.wait(s.e_mask)
            for s in streams:
                SY.now(lambda e, i, s=s: load_masks(e, s, i + turn))
            yield
            for s in streams:
                s.e_mask = act(s.sm[:, :, :], s.sm[:, :, :], ACT.Ln, after=(s.e_mask,))
            yield
            for s in streams:
                s.mask_ready = tt(PO, s.lmask[:, :, :], s.sm[:, :, :], s.lmask[:, :, :], ALU.add,
                                  after=(s.e_mask, s.e_zero))

        def cross(s, bk, wq, bq_cols, row_bk, add_bk, wo, row_o, masked):
            e_xT = transpose_tokens(s.x, s.xT, bk[0], s.x_ready)
            e_xb = add_row(s, row_o, s.x_ready)
            e_qb = const_score(s, row_bk, s.x_ready)
            if add_bk is not None:
                e_qb = ts(PO, s.qb[:, :], s.qb[:, :], add_bk[0:S, :], ALU.add, after=(e_qb,))
            yield
            last = project(wq, s.xT, bk[1], T, after=(e_xT,))
            for e in range(NC):
                if bq_cols is None:
                    ev = act(s.qT[:, e, :], bk[1].ap[:, e * T:(e + 1) * T], after=(last,))
                else:
                    ev = act(s.qT[:, e, :], bk[1].ap[:, e * T:(e + 1) * T], ACT.Identity, after=(last,),
                             bias=bq_cols[:, e:e + 1])
            bk[1].free = e_q = ev
            yield
            e_p = [None] * NB
            for b in range(NB):
                k = bk[b]
                for c in range(NC):
                    last = mm(k.ap[0:S, 0:S2], s.qT[:, c, b * S:(b + 1) * S], s.ctxT[:, b, c, :],
                              start=c == 0, stop=c == NC - 1, after=(e_q, k.free), signal=c == NC - 1)
                if masked:
                    ev = VE.put(lambda e, b=b, k=k: e.tensor_tensor_reduce(
                        out=s.sm[:, b, :], in0=k.ap[0:S, 0:S2], in1=s.lmask[:, b, :], scale=1.0, scalar=3.0 * NEG,
                        op0=ALU.add, op1=ALU.max, accum_out=s.mx2[0:S, b:b + 1]), after=(last, s.mask_ready))
                    if b == NB - 1:
                        s.masks_in_use = False
                    k.free = ev
                    src = s.sm[:, b, :]
                else:
                    ev = reduce(VE, s.mx2[0:S, b:b + 1], k.ap[0:S, 0:S2], ALU.max, after=(last,))
                    src = k.ap[0:S, 0:S2]
                ev = stt(s.nb[:, b:b + 1], s.mx2[0:S, b:b + 1], s.qb[:, b:b + 1], s.qb[:, b:b + 1],
                         ALU.add, ALU.subtract, after=(ev, e_qb), reverse1=True)
                e_p[b] = act(s.p[:, b, 0:S2], src, ACT.Exp, after=(ev,), bias=s.nb[:, b:b + 1],
                             accum_out=s.sum[:, b:b + 1])
                if masked:
                    s.mask_used = (e_p[b],)
                else:
                    k.free = e_p[b]
                yield
            e_r = recip(s.rsum[:, :], s.sum[:, :], after=(e_p[-1],))
            yield
            for b in range(NB):
                k = bk[2]
                for j in range(S2C):
                    last = tr(k.ap[:, j * S:(j + 1) * S], s.p[:, b, j * P:(j + 1) * P], ident[0:S, 0:S],
                              after=(e_p[b], k.free), signal=j == S2C - 1)
                k.free = e_pT = copy((VE, AC)[b], s.pT[:, :, :].rearrange("p j t -> p (j t)"), k.ap[:, 0:S2C * S],
                                     after=(last,))
                yield
                k = bk[3]
                for c in range(NC):
                    for j in range(S2C):
                        last = mm(k.ap[:, c * S:(c + 1) * S], s.ctx[:, b, j, c * P:(c + 1) * P], s.pT[:, j, :],
                                  start=j == 0, stop=j == S2C - 1, after=(e_pT, k.free),
                                  signal=(c, j) == (NC - 1, S2C - 1))
                k.free = e_a = copy((AC, VE)[b], s.aT[:, :, b * S:(b + 1) * S],
                                    k.ap[:, 0:NC * S].rearrange("p (c t) -> p c t", c=NC), after=(last,))
                if b == 0:
                    e_a0 = e_a
                    yield
            s.ctx_used = last
            yield
            last = project_tokens(s.aT, wo, bk[0], after=(e_a0, e_a))
            ready = [stt(s.r[:, b, :], bk[0].ap[0:S, b * D:(b + 1) * D], s.rsum[:, b:b + 1], s.xb[:, b, :],
                         ALU.mult, ALU.add, after=(last, e_r, e_xb)) for b in range(NB)]
            bk[0].free = ready[-1]
            yield
            s.x_ready = yield from layernorm(s, s.x, ready)

        def heads(s, bk, t, v, mask_w, mask_x, dst, ready):
            for k in bk:
                k.held = True
            last, part = [None] * ROWS, [slice(4 * g, 4 * g + 4) for g in range(ROWS)]
            n = mask_w.shape[0]
            for c in range(NC):
                for j in range(2):
                    for g in range(ROWS):
                        r, at = slice(32 * g, 32 * g + 32), (2 * c + j) * S
                        mm(bk[g].ap[0:S, at:at + S], s.qT[r, c, t], s.kT[r, j, c, t],
                           start=(c, j) == (0, 0), stop=False, after=(*ready, bk[g].free), shared=True)
            for g in range(ROWS):
                last[g] = mm(bk[g].ap[0:S, 0:4 * S], mask_w[:, :], mask_x[:, :].unsqueeze(1).to_broadcast([n, 4, S]),
                             start=False, stop=False, shared=True, signal=True)
            for g in range(ROWS):
                ev = reduce(VE, s.mx[:, part[g]], bk[g].ap[0:S, 0:4 * S].rearrange("p (q k) -> p q k", q=4),
                            ALU.max, after=(last[g],))
                if g == 1:
                    yield
            yield
            e1 = ts(VE, s.hl[:, 0:H], s.mx[:, :], -1.0, ALU.mult, after=(ev,))
            e1 = stt(s.hl[:, H:2 * H], s.mx[:, :], -1.0, s.hl[:, 0:H], ALU.mult, ALU.subtract, after=(e1,))
            row = bk[3].ap[0:2 * H, 4 * S:5 * S]
            e1 = mm(row, s.hl[:, :], ident_b[0:S, 0:S], start=False, stop=False, after=(e1,), signal=True, shared=True)
            e1 = copy(VE, s.shift[:, :], row, after=(e1,))
            yield
            for g in range(ROWS):
                e_s = mm(bk[g].ap[0:S, 0:4 * S], s.shift[:, :], pick_head[:, part[g], :], start=False, stop=True,
                         after=(e1, ev), shared=True, signal=True)
                e_e = act(s.e[0:S, part[g], :].rearrange("p q k -> p (q k)"), bk[g].ap[0:S, 0:4 * S], ACT.Exp,
                          after=(e_s,), scale=float(DH) ** -0.5)
                bk[g].free, bk[g].held = e_e, False
                last[g] = reduce(VE, s.den[:, part[g]], s.e[0:S, part[g], :], ALU.add, after=(e_e,))
                if g % 2:
                    yield
            for g in range(ROWS):
                ev = recip(s.rden[:, part[g]], s.den[:, part[g]], after=(last[g],))
                last[g] = tt(VE, s.e[0:S, part[g], :], s.e[0:S, part[g], :],
                             s.rden[:, part[g]].unsqueeze(2).to_broadcast([S, 4, S]), ALU.mult, after=(ev,))
                if g == 1:
                    yield
            for g in range(ROWS):
                if g > 0:
                    yield
                for q in range(4):
                    e_t = tr(bk[g].ap[0:S, q * S:(q + 1) * S], s.e[0:S, 4 * g + q, :], ident[0:S, 0:S],
                             after=(last[g], bk[g].free), signal=q == 3)
                bk[g].free = last[g] = copy((AC, VE)[g % 2], s.eT[:, part[g], :].rearrange("p q k -> p (q k)"),
                                            bk[g].ap[0:S, 0:4 * S], after=(e_t,))
            yield
            k = bk[0]
            for c in range(NC):
                for j in range(2):
                    for g in range(ROWS):
                        e_o = mm(k.ap[32 * g:32 * g + 32, c * S:(c + 1) * S], v[:, 8 * c + 2 * g + j, :],
                                 s.eT[:, 4 * g + 2 * c + j, :], start=(c, j) == (0, 0), stop=j == 1,
                                 after=(last[g], k.free), shared=True, signal=(c, j, g) == (NC - 1, 1, ROWS - 1))
            k.free = act(dst, k.ap[:, 0:NC * S].rearrange("p (c t) -> p c t", c=NC), after=(e_o,))
            return k.free

        def spread_heads(v):
            return v.rearrange("p (u j x d) -> p u (j x) d", j=2, x=2, d=DH)[:, :, 0:4:3, :]

        def sub_select(s, bk):
            for b in range(NB):
                ev = stt(s.prod[:, b, :], s.x[:, b, :], 1.0, rows["f_wg"][0:S, :], ALU.mult, ALU.mult,
                         after=(s.x_ready, s.prod_used), accum_out=s.z[:, b:b + 1])
            yield
            ev = act(s.ez[:, :], s.z[:, :], ACT.Exp, after=(ev,), scale=-1.0)
            ev = ts(VE, s.gp[:, :], s.ez[:, :], 1.0, ALU.add, after=(ev,))
            e_g = recip(s.gate[:, :], s.gp[:, :], after=(ev,))
            for b in range(NB):
                e_d = ts(VE, s.dg[:, b, :], ident[0:S, 0:S], s.gate[:, b:b + 1], ALU.mult, after=(e_g,))
            yield
            last = mm(bk[0].ap[0:S, 0:T], ones[0:S, 0:S], s.dg[:, :, :].rearrange("p b t -> p (b t)"),
                      after=(e_d, bk[0].free), signal=True)
            for b in range(NB):
                gates = bk[0].ap[0:S, b * S:(b + 1) * S]
                ev = stt(s.tie[:, :], gates, s.gate[:, b:b + 1], before[:, :], ALU.is_equal, ALU.mult,
                         after=(last, VE_last()))
                ev = stt(s.above[:, :], gates, s.gate[:, b:b + 1], s.tie[:, :], ALU.is_gt, ALU.add,
                         after=(ev,), accum_out=s.rank[:, b:b + 1])
            bk[0].free = ev
            for b in range(NB):
                e_s = ts(VE, s.sel[:, b, :], slots[:, b, :], s.rank[:, b:b + 1], ALU.is_equal, after=(ev,))
            yield
            for b in range(NB):
                tr(bk[1].ap[0:S, b * S:(b + 1) * S], s.sel[:, b, :], ident[0:S, 0:S], after=(e_s, bk[1].free))
            for c in range(NC):
                for b in range(NB):
                    last = mm(bk[1].ap[:, (2 + c) * S:(3 + c) * S], s.x[:, b, c * P:(c + 1) * P], s.sel[:, b, :],
                              start=b == 0, stop=b == NB - 1, signal=(c, b) == (NC - 1, NB - 1))
            t = slice(0, S)
            e_sT = act(s.xT[:, :, t], bk[1].ap[:, 2 * S:4 * S].rearrange("p (c m) -> p c m", c=NC), after=(last,))
            bk[1].free = e_selT = act(s.selT[:, :, :].rearrange("p b m -> p (b m)"), bk[1].ap[0:S, 0:NB * S],
                                      after=(last,))
            yield
            last = project(W["f_q"], s.xT, bk[2], S, after=(e_sT,))
            bk[2].free = e_q = act(s.qT[:, :, t], bk[2].ap[:, 0:NC * S].rearrange("p (c m) -> p c m", c=NC),
                                   after=(last,))
            yield
            last = project(W["f_k"], s.xT, bk[3], S)
            for j in range(2):
                e_k = ts(VE, s.kT[:, j, :, t], bk[3].ap[:, 0:NC * S].rearrange("p (c m) -> p c m", c=NC),
                         parity[:, j:j + 1], ALU.mult, after=(last,))
            bk[3].free = e_k
            yield
            for c in range(NC):
                last = mm(bk[0].ap[0:S, 0:D], s.xT[:, c, t], W["f_v"][:, c, :], start=c == 0, stop=c == NC - 1,
                          after=(bk[0].free,), signal=c == NC - 1)
            bk[0].free = e_v = act(spread_heads(s.v[:, 0, :, :].rearrange("p h d -> p (h d)")),
                                   bk[0].ap[0:S, 0:D].rearrange("p (u j d) -> p u j d", j=2, d=DH), after=(last,))
            yield
            ev = yield from heads(s, bk, t, s.v[:, 0, :, :], pair_w, pair_x, s.aT[:, :, t], (e_q, e_k, e_v))
            yield
            for c in range(NC):
                last = mm(bk[2].ap[0:S, 0:D], s.aT[:, c, t], W["f_o"][:, c, :], start=c == 0, stop=c == NC - 1,
                          after=(ev, bk[2].free), signal=c == NC - 1)
            bk[2].free = ev = act(s.w0[:, :], bk[2].ap[0:S, 0:D], after=(last,))
            yield
            for b in range(NB):
                last = mm(bk[3].ap[0:S, b * D:(b + 1) * D], s.selT[:, b, :], s.w0[:, :],
                          after=(ev, e_selT, bk[3].free), signal=b == NB - 1)
            ready = [stt(s.r[:, b, :], bk[3].ap[0:S, b * D:(b + 1) * D], s.gate[:, b:b + 1], s.x[:, b, :],
                         ALU.mult, ALU.add, after=(last,)) for b in range(NB)]
            bk[3].free = ready[-1]
            yield
            s.x_ready = yield from layernorm(s, s.x, ready)

        def sub_local(s, bk):
            e_xT = transpose_tokens(s.x, s.xT, bk[0], s.x_ready)
            e_xb = add_row(s, bo1, s.x_ready)
            yield
            last = project(W["a_q"], s.xT, bk[1], T, after=(e_xT,))
            for e in range(NC):
                e_q = act(s.qT[:, e, :], bk[1].ap[:, e * T:(e + 1) * T], ACT.Identity, after=(last,),
                          bias=cols["a_bq"][:, e:e + 1])
            bk[1].free = e_q
            yield
            last = project(W["a_k"], s.xT, bk[2], T)
            for j in range(2):
                for e in range(NC):
                    e_k = ts(VE, s.kT[:, j, e, :], bk[2].ap[:, e * T:(e + 1) * T], parity[:, j:j + 1], ALU.mult,
                             bkp[:, j, e:e + 1], ALU.add, after=(last,))
            bk[2].free = e_k
            yield
            last = project_tokens(s.xT, W["a_v"], bk[3])
            bk[3].free = e_v = act(spread_heads(s.v[:, :, :, :].rearrange("p b h d -> p (b h d)")),
                                   bk[3].ap[0:S, 0:NB * D].rearrange("p (u j d) -> p u j d", j=2, d=DH), after=(last,))
            yield
            e_oT = None
            for b in range(NB):
                t = slice(b * S, (b + 1) * S)
                e_oT = yield from heads(s, bk, t, s.v[:, b, :, :], band_w, band_x, s.aT[:, :, t], (e_q, e_k, e_v))
                yield
            last = project_tokens(s.aT, W["a_o"], bk[2], after=(e_oT,))
            ev = tt(VE, s.r[:, :, :].rearrange("p b d -> p (b d)"), bk[2].ap[0:S, 0:NB * D],
                    s.xb[:, :, :].rearrange("p b d -> p (b d)"), ALU.add, after=(last, e_xb))
            bk[2].free = ev
            yield
            s.x_ready = yield from layernorm(s, s.x, [ev, ev])

        def sub_quant(s, bk):
            e_xb = add_row(s, rows["n_bias"], s.x_ready)
            for b in range(NB):
                e_ms = act(s.prod[:, b, :], s.x[:, b, :], ACT.Square, after=(s.x_ready,),
                           accum_out=s.ms[:, b:b + 1])
            e_am = act(s.r[:, :, :], s.x[:, :, :], ACT.Abs, after=(s.x_ready,))
            e_am = reduce(VE, s.am[:, :], s.r[:, :, :], ALU.max, after=(e_am,))
            yield
            ev = ts(PO, s.ms[:, :], s.ms[:, :], 1.0 / D, ALU.mult, RMS_EPS, ALU.add, after=(e_ms,))
            ev = tt(PO, s.rms[:, :], s.ms[:, :], minus_half[0:S, 0:NB], ALU.pow, after=(ev,))
            yield
            ev = tt(VE, s.am2[:, :], s.am[:, :], s.rms[:, :], ALU.mult, after=(ev, e_am))
            ev = ts(VE, s.am2[:, :], s.am2[:, :], ACT_EPS, ALU.max, after=(ev,))
            e_os = ts(VE, s.os[:, :], s.am2[:, :], qscale[0:S, :], ALU.mult, after=(ev,))
            ev = recip(s.ra[:, :], s.am2[:, :], after=(ev,))
            ev = ts(VE, s.sc[:, :], s.ra[:, :], 127.0, ALU.mult, after=(ev,))
            for b in range(NB):
                e1 = ts(VE, s.y[:, b, :], s.x[:, b, :], s.rms[:, b:b + 1], ALU.mult, s.sc[:, b:b + 1], ALU.mult,
                        after=(ev,))
            e1 = ts(VE, s.y[:, :, :], s.y[:, :, :], ROUND, ALU.add, ROUND + 127.0, ALU.min, after=(e1,))
            e1 = ts(VE, s.yq[:, :, :], s.y[:, :, :], ROUND - 128.0, ALU.max, ROUND, ALU.subtract, after=(e1,))
            yield
            for c in range(NC):
                for b in range(NB):
                    at = (c * NB + b) * S
                    last = tr(bk[0].bf[:, at:at + S], s.yq[:, b, c * P:(c + 1) * P], ident_b[0:S, 0:S],
                              after=(e1, bk[0].free), signal=(c, b) == (NC - 1, NB - 1))
            bk[0].free = ev = act(s.yT[:, :, :].rearrange("p c t -> p (c t)"), bk[0].bf[:, 0:NC * T], after=(last,))
            yield
            last = project_tokens(s.yT, w8, bk[1], after=(ev,))
            ready = [stt(s.r[:, b, :], bk[1].ap[0:S, b * D:(b + 1) * D], s.os[:, b:b + 1], s.xb[:, b, :],
                         ALU.mult, ALU.add, after=(last, e_os, e_xb)) for b in range(NB)]
            bk[1].free = ready[-1]
            yield
            VE.now(lambda e, i: e.wait_ge(s_store[s.n], 16 * (i + 1)))
            s.x_ready = yield from layernorm(s, s.out, ready)

        def store(s, tile):
            SY.wait(s.x_ready)
            SY.now(lambda e, i: e.dma_start(out[bass.ds(i * 2 + s.n, 1), :, :, :].rearrange("o p b d -> (o p) b d"),
                                            tile[:, :, :]).then_inc(s_store[s.n], 16))

        def load_group(e, turn):
            e.dma_start(xin[:, :, :], ins["x"][turn, :, :, :].rearrange("p b d -> p b d")
                        if isinstance(turn, int) else
                        ins["x"][bass.ds(turn, 1), :, :, :].rearrange("o p b d -> (o p) b d")).then_inc(s_xin, 16)

        def pick(name, n, turn):
            if isinstance(turn, int):
                return ins[name][turn * 2 + n, :, :, :]
            return ins[name][bass.ds(turn * 2 + n, 1), :, :, :].rearrange("o p b d -> (o p) b d")

        def load_masks(e, s, turn):
            e.dma_start(s.cell[:, :, :], pick("cell", s.n, turn)).then_inc(s_mask[s.n], 16)
            src = ins["seq"][turn * 2 + s.n:turn * 2 + s.n + 1, :] if isinstance(turn, int) else \
                ins["seq"][bass.ds(turn * 2 + s.n, 1), :]
            e.dma_start(s.seq[:, :, :].rearrange("p b k -> p (b k)"),
                        src.to_broadcast([S, NB * S2])).then_inc(s_mask[s.n], 16)

        def load_ctx(e, s, turn):
            e.dma_start(s.ctxT[:, :, :, :].rearrange("p b c k -> p b (c k)"),
                        pick("ctxT", s.n, turn)).then_inc(s_ctx[s.n], 16)
            e.dma_start(s.ctx[:, :, :, :].rearrange("p b j d -> p b (j d)"),
                        pick("ctx", s.n, turn)).then_inc(s_ctx[s.n], 16)

        def first_part(s, bk, turn):
            while s_tok[2] == 0:
                yield
            yield from sub_agent(s, bk)
            s.took = True
            yield
            while s.mask_ready is None and turn == 2:
                yield
            PE.now(lambda e, i: e.wait_ge(s_ctx[s.n], 32 * (i + turn)))
            yield from cross(s, bk, W["x_k"], None, rows["x_bk"], None, W["x_o"], rows["x_bo"], True)
            yield

        def last_part(s, bk):
            yield from sub_select(s, bk)
            yield
            yield from sub_local(s, bk)
            yield
            yield from cross(s, bk, wqk, bqk, wqbk, bqbk, wvo, bvo, False)
            SY.wait(s.ctx_used)
            SY.now(lambda e, i: load_ctx(e, s, i + 1))
            yield
            yield from sub_quant(s, bk)
            store(s, s.out)
            yield

        def stream_a(s):
            bk = banks[0:4]
            yield from first_part(s, bk, 1)
            yield from last_part(s, bk)

        def stream_b(s):
            bk = banks[4:8]
            yield from last_part(s, bk)
            while s_tok[2] < 2:
                yield
            yield from first_part(s, bk, 2)

        def agent_next():
            while not streams[0].took:
                yield
            kept = streams[0].agent_used
            SY.wait(*kept)
            SY.now(lambda e, i: load_group(e, i + 1))
            yield
            yield from agent(lambda e, i: e.wait_ge(s_xin, 16 * (i + 2)), kept)
            s_tok[2] = 2

        n_const = 0

        def load(dst, src):
            nonlocal n_const
            n_const += 16
            SY.now(lambda e, i: e.dma_start(dst, src).then_inc(s_const, 16))

        SY.now(lambda e, i: load_group(e, 0))
        for n in WEIGHTS:
            load(W[n][:, :, :], ins[n].rearrange("(c p) n -> p c n", p=P))
        for n in ROWVECS:
            load(rows[n][:, :], ins[n].to_broadcast([P, D]))
        for n in COLVECS:
            load(cols[n][:, :], ins[n])
        load(w8_i, ins["w8"].rearrange("(c p) n -> p c n", p=P))
        load(wscale[:, :], ins["wscale"].to_broadcast([P, 1]))
        for n, t in (("ident", ident), ("ident_b", ident_b), ("before", before), ("parity", parity),
                     ("band_w", band_w), ("band_x", band_x), ("pair_w", pair_w), ("pair_x", pair_x)):
            load(t[:, :], ins[n])
        for n, t in (("pick_batch", pick_batch), ("pick_head", pick_head), ("slots", slots), ("only", only)):
            load(t[:, :, :], ins[n])
        for s in streams:
            SY.now(lambda e, i, s=s: load_masks(e, s, 0))
            SY.now(lambda e, i, s=s: load_ctx(e, s, 0))
            SY.now(lambda e, i, s=s: e.sem_inc(s_store[s.n], 16))

        VE.put(lambda e: e.memset(ones[:, :], 1.0))
        VE.put(lambda e: e.memset(minus_half[:, :], -0.5))
        for s in streams:
            VE.put(lambda e, s=s: e.memset(s.p[:, :, :], 0.0))
            VE.put(lambda e, s=s: e.memset(s.v[:, :, :, :], 0.0))
        for q in (VE, PE, AC, PO):
            q.now(lambda e, i: e.wait_ge(s_const, n_const))

        def spread(bank, vec, w, at=0, cols_=D):
            for c in range(NC):
                last = mm(bank.ap[:, at:at + cols_], vec[:, c:c + 1].to_broadcast([P, P]), w[:, c, 0:cols_],
                          start=c == 0, stop=c == NC - 1, after=(bank.free,), signal=c == NC - 1)
            return last

        inv = float(D) ** -0.5
        last = spread(banks[0], cols["w_conv1"], W["w_q0"])
        banks[0].free = e_aw = copy(VE, agent_w[:, :], banks[0].ap[:, 0:D], after=(last,))
        last = spread(banks[1], cols["a_bv"], W["a_o"])
        banks[1].free = tt(VE, bo1[:, :], banks[1].ap[:, 0:D], rows["a_bo"][:, :], ALU.add, after=(last,))
        last = spread(banks[2], cols["c_bk"], W["c_qT"])
        banks[2].free = ts(VE, wqbk[:, :], banks[2].ap[:, 0:D], inv, ALU.mult, after=(last,))
        last = spread(banks[4], cols["c_bv"], W["c_o"])
        banks[4].free = tt(VE, bvo[:, :], banks[4].ap[:, 0:D], rows["c_bo"][:, :], ALU.add, after=(last,))
        for c in range(NC):
            last = mm(banks[5].ap[:, 0:1], cols["c_bk"][:, c:c + 1].to_broadcast([P, P]), cols["c_bq"][:, c:c + 1],
                      start=c == 0, stop=c == NC - 1, after=(banks[5].free,), signal=c == NC - 1)
        banks[5].free = ts(VE, bqbk[:, :], banks[5].ap[:, 0:1], inv, ALU.mult, after=(last,))
        for e in range(NC):
            for c in range(NC):
                last = mm(banks[6].ap[:, e:e + 1], W["c_kT"][:, c, e * P:(e + 1) * P], cols["c_bq"][:, c:c + 1],
                          start=c == 0, stop=c == NC - 1, signal=(e, c) == (NC - 1, NC - 1))
        banks[6].free = ts(VE, bqk[:, :], banks[6].ap[:, 0:NC], inv, ALU.mult, after=(last,))
        for dst, a, b_, scale in ((wqk, W["c_qT"], W["c_kT"], inv), (wvo, W["c_vT"], W["c_o"], 1.0)):
            for e in range(NC):
                for c in range(NC):
                    last = mm(banks[7].ap[:, e * D:(e + 1) * D], a[:, c, e * P:(e + 1) * P], b_[:, c, :],
                              start=c == 0, stop=c == NC - 1, after=(banks[7].free,), signal=(e, c) == (NC - 1, NC - 1))
            banks[7].free = ts(VE, dst[:, :, :].rearrange("p c n -> p (c n)"), banks[7].ap[:, 0:NC * D], scale,
                               ALU.mult, after=(last,))
        for j in range(2):
            ts(VE, bkp[:, j, :], cols["a_bk"][:, :], parity[:, j:j + 1], ALU.mult)
        copy(VE, w8[:, :, :], w8_i)
        ts(VE, qscale[:, :], wscale[:, :], 1.0 / 127.0, ALU.mult)
        VE.wait(e_aw)
        for _ in agent(lambda e, i: e.wait_ge(s_xin, 16), ()):
            pass
        for _ in log_masks(1):
            pass
        for _ in first_part(streams[1], banks[4:8], 1):
            pass

        prologue = {q.name: list(q.steps) for q in (*engines, SY)}
        prologue_counts = {q.name: q.count for q in engines}
        for q in (*engines, SY):
            q.restart()
        for k in banks:
            k.free = None

        for s in streams:
            s.took, s.prod_used, s.x_ready, s.mask_ready, s.mask_used = False, None, None, None, ()
        streams[0].masks_in_use = True
        s_tok[:] = [None, None, 1]
        steps = {"A": stream_a(streams[0]), "B": stream_b(streams[1]), "N": agent_next(),
                 "M": log_masks(2)}
        for name in ORDER:
            next(steps[name], None)
        for step in steps.values():
            assert next(step, None) is None and next(step, "end") == "end", "ORDER is too short"
        body_counts = {q.name: q.count for q in engines}

        def meet(e, q, counts):
            if q in engines:
                e.wait_ge(q.sem, counts[q.name])
            if q is PO:
                e.wait_ge(s_arrive, len(s_go))
                for other in engines:
                    e.sem_clear(other.sem)
                e.sem_clear(s_arrive)
                for n in s_go:
                    e.sem_inc(s_go[n], 1)
            else:
                e.sem_inc(s_arrive, 1)
                e.wait_ge(s_go[q.name], 1)
                e.sem_clear(s_go[q.name])

        def emit(e, q):
            for step in prologue[q.name]:
                step(e, 0)
            meet(e, q, prologue_counts)
            with e.Fori(0, NI) as i:
                q.run(e, i)
                meet(e, q, body_counts)
            if q is SY:
                for s in streams:
                    e.wait_ge(s_store[s.n], 16 * (NI + 1))
                    e.wait_ge(s_mask[s.n], 32 * (NI + 2))
                    e.wait_ge(s_ctx[s.n], 32 * (NI + 1))
                e.wait_ge(s_xin, 16 * (NI + 1))

        block = ctx.enter_context(nc.Block())

        @block.sync
        def _(e):
            emit(e, SY)

        @block.gpsimd
        def _(e):
            emit(e, PO)

        @block.scalar
        def _(e):
            emit(e, AC)

        @block.tensor
        def _(e):
            emit(e, PE)

        @block.vector
        def _(e):
            emit(e, VE)


ORDER = ("BBBAAABBNNBANANNANBNABANAABABNABBBAANNNNBABNABMBNABABBABNBMAAABAABAAANABBAABABBABBBABABABBAABMABABBB"
         "BBAABBAABABAABAAABAABABBBAABBABBAABBMMABAABAABBABBAABBAABABBBAAAAABBABABAABBBBAABABBABABAABBAA")
WEIGHTS = ["w_q0", "w_k0", "w_v0", "w_v0T", "x_k", "x_o", "f_q", "f_k", "f_v", "f_o", "a_q", "a_k", "a_v", "a_o",
           "c_qT", "c_kT", "c_vT", "c_o"]
EARLY = ["c_qT", "c_kT", "c_vT", "w_q0", "c_o", "w8_i"]
ROWVECS = ["x_bk", "x_bo", "f_wg", "a_bo", "c_bo", "n_bias"]
COLVECS = ["w_conv1", "a_bq", "a_bk", "a_bv", "c_bq", "c_bk", "c_bv"]


def constants():
    bf = mybir.dt.np(BF16)
    t = np.arange(S)
    edge = np.concatenate([np.arange(NEDGE), np.arange(S - NEDGE, S)])
    one_key = (edge[:, None] == t[None, :]).astype(np.float32)
    mask = np.where(np.abs(edge[:, None] - t[None, :]) > BAND, NEG, 0.0).astype(np.float32)
    head = np.zeros((2 * H, H, S), np.float32)
    for h in range(H):
        head[h, h] = head[H + h, h] = 1.0
    slots = np.full((S, NB, S), -1.0, np.float32)
    for b in range(NB):
        slots[:, b, b * CAP:(b + 1) * CAP] = np.arange(CAP)
    batch = t // CAP == np.arange(P)[:, None]
    pick = np.zeros((G, G, S), np.float32)
    for b in range(G):
        pick[b, b] = 1.0
    row = np.arange(P) // DH % 2
    return {
        "ident": np.eye(P, dtype=np.float32), "ident_b": np.eye(P).astype(bf),
        "before": (t[None, :] < t[:, None]).astype(np.float32), "slots": slots,
        "parity": np.stack([row == 0, row == 1], 1).astype(np.float32),
        "only": np.tile(np.eye(G, dtype=np.float32), (P, 1, 1)),
        "pick_batch": pick, "pick_head": head.astype(bf),
        "band_w": one_key.astype(bf), "band_x": mask.astype(bf),
        "pair_w": batch.astype(bf), "pair_x": np.where(batch | (np.arange(P)[:, None] >= NB), 0.0, NEG).astype(bf),
    }


def kernel(x, ctx_1024, mask_BxSxS2_ff1, mask_BxS2_ff1, L0_attn_w_qkv, L0_attn_w_conv1, L0_xattn_W_k, L0_xattn_b_k,
           L0_xattn_W_o, L0_xattn_b_o, L0_ffn_Wg, L0_ffn_Wq, L0_ffn_Wk, L0_ffn_Wv, L0_ffn_Wo, L1_attn_Wq, L1_attn_bq,
           L1_attn_Wk, L1_attn_bk, L1_attn_Wv, L1_attn_bv, L1_attn_Wo, L1_attn_bo, L1_xattn_Wq, L1_xattn_bq,
           L1_xattn_Wk, L1_xattn_bk, L1_xattn_Wv, L1_xattn_bv, L1_xattn_Wo, L1_xattn_bo, L1_ffn_w_int8,
           L1_ffn_weight_scale, L1_ffn_bias):
    import concourse.bacc as _bacc
    from concourse.bass_utils import run_bass_kernel_spmd as _run

    def arr(a):
        return np.ascontiguousarray(np.asarray(a))

    def more(a):
        return np.concatenate([a, a[:2 * G]], 0)

    x, c = arr(x), arr(ctx_1024)
    cpad = np.zeros((B, S2C * P, D), c.dtype)
    cpad[:, :S2] = c
    w = arr(L0_attn_w_qkv)

    def streams_first(a):
        a = more(a).reshape(-1, NB, *a.shape[1:])
        return arr(np.moveaxis(a, 1, 2))

    def col(v):
        return arr(arr(v).reshape(NC, P).T)

    def row(v):
        return arr(v).reshape(1, D)

    arrays = {
        "x": arr(np.moveaxis(more(x).reshape(-1, G, S, D), 1, 2)),
        "ctx": streams_first(cpad.reshape(B, S2C, P, D).transpose(0, 2, 1, 3).reshape(B, P, S2C * D)),
        "ctxT": streams_first(c.transpose(0, 2, 1).reshape(B, NC, P, S2).transpose(0, 2, 1, 3).reshape(B, P, NC * S2)),
        "cell": streams_first(arr(mask_BxSxS2_ff1)),
        "seq": arr(more(arr(mask_BxS2_ff1)).reshape(-1, NB * S2)),
        "w_q0": w[:D], "w_k0": w[D:2 * D].T, "w_v0": w[2 * D:], "w_v0T": w[2 * D:].T,
        "x_k": L0_xattn_W_k, "x_o": arr(L0_xattn_W_o).T,
        "f_q": L0_ffn_Wq, "f_k": L0_ffn_Wk, "f_v": L0_ffn_Wv, "f_o": L0_ffn_Wo,
        "a_q": arr(L1_attn_Wq).T, "a_k": arr(L1_attn_Wk).T, "a_v": arr(L1_attn_Wv).T, "a_o": arr(L1_attn_Wo).T,
        "c_qT": arr(L1_xattn_Wq).T, "c_kT": arr(L1_xattn_Wk).T, "c_vT": arr(L1_xattn_Wv).T, "c_o": L1_xattn_Wo,
        "x_bk": row(L0_xattn_b_k), "x_bo": row(L0_xattn_b_o), "f_wg": row(L0_ffn_Wg), "a_bo": row(L1_attn_bo),
        "c_bo": row(L1_xattn_bo), "n_bias": row(L1_ffn_bias),
        "w_conv1": col(L0_attn_w_conv1), "a_bq": col(L1_attn_bq), "a_bk": col(L1_attn_bk), "a_bv": col(L1_attn_bv),
        "c_bq": col(L1_xattn_bq), "c_bk": col(L1_xattn_bk), "c_bv": col(L1_xattn_bv),
        "w8": arr(L1_ffn_w_int8).T, "wscale": arr(L1_ffn_weight_scale).reshape(1, 1),
        **constants(),
    }
    nc = _bacc.Bacc("TRN2", target_bir_lowering=False, num_devices=1)
    ins, data = {}, {}
    for name, a in arrays.items():
        a = arr(a)
        data["in_" + name] = a
        ins[name] = nc.dram_tensor("in_" + name, a.shape, mybir.dt.from_np(a.dtype), kind="ExternalInput").ap()
    out = nc.dram_tensor("out", (B // NB, S, NB, D), F32, kind="ExternalOutput").ap()
    program(nc, ins, out)
    r = _run(nc, [data], core_ids=[0])
    got = arr(r.results[0]["out"])
    return arr(np.moveaxis(got, 2, 1)).reshape(B, S, D)
```
